# Optimizing a Trainium2 kernel written in Bass

```python
import numpy as np
import jax
import jax.numpy as jnp

def _softmax(x, axis=-1):
    return jax.nn.softmax(x, axis=axis)

def _gelu(x):
    return jax.nn.gelu(x, approximate=True)

def _silu(x):
    return jax.nn.silu(x)

def _sigmoid(x):
    return jax.nn.sigmoid(x)

def _layernorm(x, axis=-1, eps=1e-05):
    m = jnp.mean(x, axis=axis, keepdims=True)
    v = jnp.var(x, axis=axis, keepdims=True)
    return (x - m) / jnp.sqrt(v + eps)

def _scatter_add(tgt, idx, src, axis=0):
    return tgt.at[idx].add(src)

def _segment_sum(src, seg, n):
    return jax.ops.segment_sum(src, seg, n)
kernel_name = 'mk_seq_preln_d1_jaxref_r8_5d24b1'

def setup_inputs(seed: int=0):
    np.random.seed(seed)
    _w = jnp.asarray

    def _L0_attn_setup():
        import jax, jax.numpy as jnp
        import numpy as np
        import math
        B, N, D = (2, 512, 128)
        NUM_LAYERS = 12
        INIT_RANGE = 0.02
        key = jax.random.key(seed)
        k1, k2 = jax.random.split(key)
        hidden_states = jax.random.normal(k1, (B, N, D), dtype=jnp.float32)
        std = INIT_RANGE / math.sqrt(2.0 * NUM_LAYERS * D)
        queries = jax.random.normal(k2, (D, D), dtype=jnp.float32) * std
        return {'hidden_states': hidden_states, 'queries': queries}
    _L0_attn_in = _L0_attn_setup()

    def _L0_ffn_setup():
        import jax, jax.numpy as jnp
        import numpy as np
        HID = 128
        NH = 16
        NKV = 4
        HD = HID // NH
        E = 8
        TOPK = 2
        FFN = 256
        EPS = 1e-05
        THETA = 10000.0

        def _rmsnorm(x, w):
            var = jnp.mean(x * x, axis=-1, keepdims=True)
            return x * jax.lax.rsqrt(var + EPS) * w

        def _rope_tables(S):
            inv_freq = 1.0 / THETA ** (jnp.arange(0, HD, 2, dtype=jnp.float32) / HD)
            freqs = jnp.arange(S, dtype=jnp.float32)[:, None] * inv_freq[None, :]
            emb = jnp.concatenate([freqs, freqs], axis=-1)
            return (jnp.cos(emb), jnp.sin(emb))

        def _apply_rope(t, cos, sin):
            t1, t2 = jnp.split(t, 2, axis=-1)
            rot = jnp.concatenate([-t2, t1], axis=-1)
            return t * cos[None, :, None, :] + rot * sin[None, :, None, :]
        key = jax.random.key(seed)
        ks = jax.random.split(key, 6)
        B, S = (1, 256)
        x = jax.random.normal(ks[0], (B, S, HID), dtype=jnp.float32)
        wqkv = jax.random.normal(ks[1], ((NH + 2 * NKV) * HD, HID), dtype=jnp.float32) * 0.02
        wo = jax.random.normal(ks[2], (HID, NH * HD), dtype=jnp.float32) * 0.02
        gate_w = jax.random.normal(ks[3], (E, HID), dtype=jnp.float32) * 0.02
        w13 = jax.random.normal(ks[4], (E, 2 * FFN, HID), dtype=jnp.float32) * 0.02
        w2 = jax.random.normal(ks[5], (E, HID, FFN), dtype=jnp.float32) * 0.02
        return {'x': x, 'ln1_w': jnp.ones((HID,), jnp.float32), 'ln2_w': jnp.ones((HID,), jnp.float32), 'wqkv': wqkv, 'wo': wo, 'gate_w': gate_w, 'w13': w13, 'w2': w2}
    _L0_ffn_in = _L0_ffn_setup()
    _d = {'L0_attn_hidden_states': _L0_attn_in['hidden_states'], 'L0_attn_queries': _L0_attn_in['queries'], 'L0_ffn_ln1_w': _L0_ffn_in['ln1_w'], 'L0_ffn_ln2_w': _L0_ffn_in['ln2_w'], 'L0_ffn_wqkv': _L0_ffn_in['wqkv'], 'L0_ffn_wo': _L0_ffn_in['wo'], 'L0_ffn_gate_w': _L0_ffn_in['gate_w'], 'L0_ffn_w13': _L0_ffn_in['w13'], 'L0_ffn_w2': _L0_ffn_in['w2']}
    _x0 = _d['L0_attn_hidden_states']
    _d['L0_attn_hidden_states'] = jax.random.normal(jax.random.fold_in(jax.random.key(seed), 1), (2, 1024, 128), dtype=_x0.dtype)
    del _x0
    return _d

def reference(L0_attn_hidden_states, L0_attn_queries, L0_ffn_ln1_w, L0_ffn_ln2_w, L0_ffn_wqkv, L0_ffn_wo, L0_ffn_gate_w, L0_ffn_w13, L0_ffn_w2):

    def _L0_attn_ref(hidden_states, queries):
        import jax, jax.numpy as jnp
        import numpy as np
        import math
        B, N, D = (2, 512, 128)
        NUM_LAYERS = 12
        INIT_RANGE = 0.02
        q = jnp.einsum('bnd,ed->bne', hidden_states, queries)
        pre_attn = jnp.einsum('bne,bme->bnm', q, hidden_states)
        attention = jnp.einsum('bnm,bmd->bnd', pre_attn, hidden_states)
        return attention

    def _L0_ffn_ref(x, ln1_w, ln2_w, wqkv, wo, gate_w, w13, w2):
        import jax, jax.numpy as jnp
        import numpy as np
        HID = 128
        NH = 16
        NKV = 4
        HD = HID // NH
        E = 8
        TOPK = 2
        FFN = 256
        EPS = 1e-05
        THETA = 10000.0

        def _rmsnorm(x, w):
            var = jnp.mean(x * x, axis=-1, keepdims=True)
            return x * jax.lax.rsqrt(var + EPS) * w

        def _rope_tables(S):
            inv_freq = 1.0 / THETA ** (jnp.arange(0, HD, 2, dtype=jnp.float32) / HD)
            freqs = jnp.arange(S, dtype=jnp.float32)[:, None] * inv_freq[None, :]
            emb = jnp.concatenate([freqs, freqs], axis=-1)
            return (jnp.cos(emb), jnp.sin(emb))

        def _apply_rope(t, cos, sin):
            t1, t2 = jnp.split(t, 2, axis=-1)
            rot = jnp.concatenate([-t2, t1], axis=-1)
            return t * cos[None, :, None, :] + rot * sin[None, :, None, :]
        B, S, _ = x.shape
        h = _rmsnorm(x, ln1_w)
        qkv = jnp.einsum('bsh,oh->bso', h, wqkv)
        q = qkv[..., :NH * HD].reshape(B, S, NH, HD)
        k = qkv[..., NH * HD:(NH + NKV) * HD].reshape(B, S, NKV, HD)
        v = qkv[..., (NH + NKV) * HD:].reshape(B, S, NKV, HD)
        cos, sin = _rope_tables(S)
        q = _apply_rope(q, cos, sin)
        k = _apply_rope(k, cos, sin)
        groups = NH // NKV
        k = jnp.repeat(k, groups, axis=2)
        v = jnp.repeat(v, groups, axis=2)
        scale = HD ** (-0.5)
        scores = jnp.einsum('bqhd,bkhd->bhqk', q, k) * scale
        causal = jnp.tril(jnp.ones((S, S), dtype=bool))
        scores = jnp.where(causal[None, None], scores, jnp.finfo(scores.dtype).min)
        probs = jax.nn.softmax(scores, axis=-1)
        attn = jnp.einsum('bhqk,bkhd->bqhd', probs, v).reshape(B, S, NH * HD)
        x = x + jnp.einsum('bso,ho->bsh', attn, wo)
        h = _rmsnorm(x, ln2_w).reshape(-1, HID)
        T = h.shape[0]
        logits = jnp.einsum('th,eh->te', h, gate_w)
        rprobs = jax.nn.softmax(logits.astype(jnp.float32), axis=-1)
        topw, topi = jax.lax.top_k(rprobs, TOPK)
        topw = topw / jnp.sum(topw, axis=-1, keepdims=True)
        wfull = jnp.zeros((T, E), jnp.float32).at[jnp.arange(T)[:, None], topi].set(topw)
        wfull = wfull.astype(h.dtype)
        out = jnp.zeros((T, HID), h.dtype)
        for e in range(E):
            w1 = w13[e, :FFN]
            w3 = w13[e, FFN:]
            g = jax.nn.silu(h @ w1.T) * (h @ w3.T)
            out = out + jnp.einsum('tf,hf->th', g, w2[e]) * wfull[:, e:e + 1]
        return x + out.reshape(B, S, HID)
    x = L0_attn_hidden_states
    x = x + _L0_attn_ref(_layernorm(x, axis=-1), L0_attn_queries)
    x = x + _L0_ffn_ref(_layernorm(x, axis=-1), L0_ffn_ln1_w, L0_ffn_ln2_w, L0_ffn_wqkv, L0_ffn_wo, L0_ffn_gate_w, L0_ffn_w13, L0_ffn_w2)
    return x

_drawn_inputs = setup_inputs


def setup_inputs(seed=0):
    import zlib

    import numpy as np

    out = dict(_drawn_inputs(seed))
    spreads = {'L0_ffn_ln1_w': (1.0, 0.6), 'L0_ffn_ln2_w': (1.0, 0.6)}
    factors = {'L0_ffn_wqkv': 8.0,
     'L0_ffn_wo': 8.0,
     'L0_ffn_gate_w': 8.0,
     'L0_ffn_w13': 8.0,
     'L0_ffn_w2': 8.0}
    for name, (base, spread) in spreads.items():
        noise = np.random.default_rng([zlib.crc32(name.encode()), seed]).standard_normal(out[name].shape)
        drawn = base * np.exp(spread * noise) if base else spread * noise
        out[name] = jnp.asarray(drawn.astype(out[name].dtype))
    for name, factor in factors.items():
        out[name] = (out[name] * factor).astype(out[name].dtype)
    return out
```

```python
import concourse.bass as bass
from concourse import mybir
from contextlib import ExitStack

P = 128
B, S, HID = 2, 1024, 128
NH, NKV, HD = 16, 4, 8
REP = NH // NKV
E, FFN = 8, 256
EPS = 1e-5
T = S // P
C2 = 512
NC_ = S // C2
TC = C2 // P
NG = B * NKV
QK0, RQ0, K0, RK0, V0 = 0, 128, 256, 288, 320
WQK = 352
MASKED = -3.0e38

S_UNITS = []
for _i in range(T):
    for _k0, _nb in ((0, min(_i + 1, TC)), (TC, _i + 1 - TC)):
        if _nb > 0:
            _per = TC // _nb if _nb < 3 else 1
            for _h in range(0, REP, _per):
                S_UNITS.append((_i, _k0, _nb, list(range(_h, _h + _per))))
N_LOW = sum(1 for u in S_UNITS if u[0] < TC)
AFTER_T1, AFTER_T0 = 1, N_LOW + 5
STREAM = ([("s", u) for u in S_UNITS[:AFTER_T1]] + [("t1", None)]
          + [("s", u) for u in S_UNITS[AFTER_T1:AFTER_T0]] + [("t0", None)]
          + [("s", u) for u in S_UNITS[AFTER_T0:]])
NE = len(STREAM)
assert NE % 2 == 0
UNIT_OF = [sum(1 for x in STREAM[:e] if x[0] == "s") for e in range(NE)]
SLOTS = [(c, j) for c in range(NC_) for j in range(TC * (c + 1))]
NS = len(SLOTS)
NU = 2 * NS
NPB = 6
LAG = 2


def slot_cols(c, j):
    q0 = max(0, (j - TC * c) * P)
    return q0, C2 - q0


DIAG = [j >= TC * c for c, j in SLOTS]
MASK_NO = [2 * sum(DIAG[:s]) for s in range(NS)]
NMASK = 2 * sum(DIAG)


def stream_slots():
    cost = [0.3 + (0.53 * x[1][2] * len(x[1][3]) / 4 * 1.0 if x[0] == "s" else 0.0) for x in STREAM]
    work = [slot_cols(c, j)[1] for c, j in SLOTS]
    out, e, done = [], 0, 0.0
    for s in range(NS):
        target = sum(cost) * sum(work[:s + 1]) / sum(work)
        part = []
        while e < NE and (done + cost[e] / 2 <= target or s == NS - 1):
            part.append(e)
            done += cost[e]
            e += 1
        out.append(part)
    return out


IN_SLOT = stream_slots()
TR1_SLOT, TR0_SLOT = 3, 8


def build_program(nc, x_in, queries, ln1, ln2, wqk, wo_t, gate_t, w13_t, w2_t,
                  cos_q, sin_q, cos_k, sin_k, out):
    F, FR, BF = mybir.dt.float32, mybir.dt.float32r, mybir.dt.bfloat16
    ALU, ACT, AX = mybir.AluOpType, mybir.ActivationFunctionType, mybir.AxisListType

    ctx = ExitStack()
    with ctx:
        def sb(name, shape, dt=F, scope=ctx):
            return scope.enter_context(nc.sbuf_tensor(name, shape, dt))

        def sem(name):
            return ctx.enter_context(nc.semaphore(name))

        q_scr = nc.dram_tensor("q_scr", [NG, P, S], F, kind="Internal").ap()
        k_scr = nc.dram_tensor("k_scr", [NG, 32, S], F, kind="Internal").ap()
        v_scr = nc.dram_tensor("v_scr", [NG, P, T * 32], F, kind="Internal").ap()

        x = sb("x", [P, B * T, HID])
        y = sb("y", [P, B * T, HID])
        otok = sb("otok", [P, T, NG, 32])
        w13h, w13l = sb("w13h", [P, E, 2 * FFN], FR), sb("w13l", [P, E, 2 * FFN], FR)
        w2h, w2l = sb("w2h", [P, E, 2, HID], FR), sb("w2l", [P, E, 2, HID], FR)
        w13r, w2r = sb("w13r", [P, E, 2 * FFN]), sb("w2r", [P, E, 2, HID])
        qmat = sb("qmat", [P, HID])
        ln1c, ln2c = sb("ln1c", [P, 1]), sb("ln2c", [P, 1])
        wqk_sb = sb("wqk_sb", [P, WQK])
        wo_sb = sb("wo_sb", [P, HID])
        gate_sb = sb("gate_sb", [P, E])
        ident = sb("ident", [P, P])
        ident_bf, mask_bf = sb("ident_bf", [P, P], BF), sb("mask_bf", [P, P], BF)
        tick = sb("tick", [P, 2])
        tri = sb("tri", [P, E, E])
        eps_c = sb("eps_c", [P, 1])
        stats = sb("stats", [P, B * T, 6])
        mv = sb("mv", [P, B * T, 2])
        var_t, rstd = sb("var_t", [P, B * T]), sb("rstd", [P, B * T])
        rms = sb("rms", [P, B * T])
        gate_w = sb("gate_w", [P, B * T, E])
        mx = sb("mx", [P, NC_, TC, REP])
        mx2 = sb("mx2", [P, TC, REP])
        neg = sb("neg", [P, NC_, REP, 2, TC])
        m_rows = [sb(f"m_rows{c}", [32, P]) for c in range(NC_)]
        o_sb = [sb(f"o_sb{c}", [P, C2]) for c in range(NC_)]
        o_rec = [sb(f"o_rec{c}", [P, TC, REP]) for c in range(NC_)]

        sk_stk = [sb(f"sk_stk{i}", [P, REP, S], FR) for i in range(2)]

        s_a = ExitStack()
        h_a = [sb(f"h_a{b}", [P, T, HID], F, s_a) for b in range(B)]
        ht_a = [sb(f"ht_a{b}", [P, S], F, s_a) for b in range(B)]
        g_sb = [sb(f"g_sb{b}", [P, HID], F, s_a) for b in range(B)]
        m_sb = [sb(f"m_sb{b}", [P, HID], F, s_a) for b in range(B)]
        cq, sq = sb("cq", [P, S], F, s_a), sb("sq", [P, S], F, s_a)
        ck, sk = sb("ck", [64, C2], F, s_a), sb("sk", [64, C2], F, s_a)
        t_cos, t_sin = sb("t_cos", [P, C2], F, s_a), sb("t_sin", [P, C2], F, s_a)
        q_hi, q_lo = sb("q_hi", [P, S], FR, s_a), sb("q_lo", [P, S], FR, s_a)
        k_hi, k_lo = sb("k_hi", [64, C2], FR, s_a), sb("k_lo", [64, C2], FR, s_a)
        vaug = sb("vaug", [P, NKV, T, 32], F, s_a)
        s_a.close()
        s_b = ExitStack()
        sq_stk = [sb(f"sq_stk{i}", [P, S], FR, s_b) for i in range(2)]
        tq_stk = [[sb(f"tq_stk{i}{t}", [P, S], FR, s_b) for t in range(2)] for i in range(2)]
        tk_stk = [sb(f"tk_stk{i}", [P, S], FR, s_b) for i in range(2)]
        v_stk = [sb(f"v_stk{i}", [P, T, 32], F, s_b) for i in range(2)]
        pt = sb("pt", [P, NPB, 2, C2], F, s_b)
        s_b.close()
        s_c = ExitStack()
        ot = [sb(f"ot{b}", [P, S], F, s_c) for b in range(B)]
        h2 = sb("h2", [P, B * T, HID], F, s_c)
        h2t = sb("h2t", [P, B * S], F, s_c)
        h2h, h2l = sb("h2h", [P, B * S], FR, s_c), sb("h2l", [P, B * S], FR, s_c)
        lg, ex = sb("lg", [P, T, E], F, s_c), sb("ex", [P, T, E], F, s_c)
        cmp1, cmp2 = sb("cmp1", [P, T, E, E], F, s_c), sb("cmp2", [P, T, E, E], F, s_c)
        r8 = sb("r8", [P, 2, T], F, s_c)
        silu = [sb(f"silu{i}", [P, C2], F, s_c) for i in range(2)]
        gg = [sb(f"gg{i}", [P, C2], F, s_c) for i in range(2)]
        gh = [sb(f"gh{i}", [P, C2], FR, s_c) for i in range(4)]
        gl = [sb(f"gl{i}", [P, C2], FR, s_c) for i in range(4)]
        s_c.close()

        bank = [ctx.enter_context(nc.psum_tensor(f"bank{i}", [P, C2], F)) for i in range(2)]
        pair = [ctx.enter_context(nc.psum_tensor(f"pair{i}", [P, 2, C2], F)) for i in range(2)]
        obank = [ctx.enter_context(nc.psum_tensor(f"obank{i}", [P, C2], F)) for i in range(2)]
        BK = [bank[0][:, :], bank[1][:, :], pair[0][:, 0, :], pair[0][:, 1, :],
              pair[1][:, 0, :], pair[1][:, 1, :], obank[0][:, :], obank[1][:, :]]

        ld_x = [sem(f"ld_x{b}") for b in range(B)]
        ld_w = sem("ld_w")
        ld_rope = sem("ld_rope")
        ld_moe = sem("ld_moe")
        cst = sem("cst")
        zeroed = sem("zeroed")
        vq = sem("vq")
        aq = sem("aq")
        a_var = sem("a_var")
        a_std = sem("a_std")
        a_h = sem("a_h")
        a_tr = sem("a_tr")
        a_ht = sem("a_ht")
        a_g, a_gs = sem("a_g"), sem("a_gs")
        a_m, a_ms = sem("a_m"), sem("a_ms")
        a_att, a_x1 = sem("a_att"), sem("a_x1")
        a_qk = sem("a_qk")
        a_rope = sem("a_rope")
        a_v, a_vs = sem("a_v"), sem("a_vs")
        a_sum = sem("a_sum")
        a_hi = sem("a_hi")
        a_lo = sem("a_lo")
        scr = sem("scr")
        w_hi, w_lo = sem("w_hi"), sem("w_lo")
        ld_s = [sem(f"ld_s{i}") for i in range(2)]
        ld_t = [sem(f"ld_t{i}") for i in range(2)]
        s_ready, s_free = sem("s_ready"), sem("s_free")
        m_neg = sem("m_neg")
        n_hi, n_mx = sem("n_hi"), sem("n_mx")
        n_rc = sem("n_rc")
        ld_m = [[sem(f"ld_m{c}{i}") for i in range(2)] for c in range(NC_)]
        t_done = sem("t_done")
        e_done = sem("e_done")
        k_done = sem("k_done")
        pv_done = sem("pv_done")
        o_cp = sem("o_cp")
        o_tr = sem("o_tr")
        o_nm = sem("o_nm")
        c_tr, c_cp = sem("c_tr"), sem("c_cp")
        c_wo, c_x2 = sem("c_wo"), sem("c_x2")
        c_sq, c_rt, c_h = sem("c_sq"), sem("c_rt"), sem("c_h")
        c_lg, c_lr = sem("c_lg"), sem("c_lr")
        c_sh, c_ex = sem("c_sh"), sem("c_ex")
        c_hi, c_lo, c_w = sem("c_hi"), sem("c_lo"), sem("c_w")
        d_a, d_u = sem("d_a"), sem("d_u")
        d_s, d_g = sem("d_s"), sem("d_g")
        d_hi, d_lo = sem("d_hi"), sem("d_lo")
        d_dn = sem("d_dn")
        d_acc = sem("d_acc")
        st = sem("st")
        block = ctx.enter_context(nc.Block())

        out_v = out.rearrange("b (t p) d -> (b t) p d", p=P)
        x_v = x_in.rearrange("b (t p) d -> b p t d", p=P)

        def idx(n, e):
            if isinstance(n, int) and n == 0:
                return e - (1 if e > AFTER_T1 else 0)
            return n * NE - 1 + e

        def bank_no(n, e):
            return idx(0, e) % 2 if isinstance(n, int) and n == 0 else (e + 1) % 2

        def tr_bank(b, k, c):
            return BK[4 * b + (1 if k < 4 else 2) + c]

        T0, T1 = STREAM.index(("t0", None)), STREAM.index(("t1", None))
        LAST_T1 = NE * NG - 1

        @block.sync
        def _(sp):
            sp.dma_start(x[:, 0:T, :], x_v[0]).then_inc(ld_x[0], 16)
            for dst, src in ((qmat[:, :], queries), (ln1c[:, :], ln1), (ln2c[:, :], ln2),
                             (wqk_sb[:, :], wqk), (wo_sb[:, :], wo_t), (gate_sb[:, :], gate_t)):
                sp.dma_start(dst, src).then_inc(ld_w, 16)
            sp.dma_start(x[:, T:2 * T, :], x_v[1]).then_inc(ld_x[1], 16)
            for dst, src in ((cq, cos_q), (sq, sin_q), (ck, cos_k), (sk, sin_k)):
                sp.dma_start(dst[:, :], src).then_inc(ld_rope, 16)
            sp.dma_start(w13r[:, :, :], w13_t.rearrange("e h f -> h e f")).then_inc(ld_moe, 16)
            sp.dma_start(w2r[:, :, :, :],
                         w2_t.rearrange("e (t p) h -> p e t h", p=P)).then_inc(ld_moe, 16)
            for b in range(B):
                sp.wait_ge(a_hi, 3 * b + 1)
                sp.wait_ge(a_lo, 3 * b + 1)
                for part, slots in ((k_hi, (0, 2)), (k_lo, (1, 3))):
                    for s in slots:
                        for c in range(NC_):
                            sp.dma_start(
                                k_scr[NKV * b:NKV * (b + 1), HD * s:HD * (s + 1), C2 * c:C2 * (c + 1)],
                                part[32 * c:32 * (c + 1), :].bitcast(F)).then_inc(scr, 16)
                for c in range(NC_):
                    sp.wait_ge(a_hi, 3 * b + 2 + c)
                    sp.wait_ge(a_lo, 3 * b + 2 + c)
                    qv = q_scr[NKV * b:NKV * (b + 1)].rearrange("g (h s d) n -> (g h) s d n", h=REP, s=4)
                    for part, slots in ((q_hi, (0, 1)), (q_lo, (2, 3))):
                        for s in slots:
                            sp.dma_start(qv[:, s, :, C2 * c:C2 * (c + 1)],
                                         part[:, C2 * c:C2 * (c + 1)].bitcast(F)).then_inc(scr, 16)
                sp.wait_ge(a_vs, b + 1)
                sp.dma_start(v_scr[NKV * b:NKV * (b + 1)].rearrange("g p n -> p g n"),
                             vaug[:, :, :, :].rearrange("p g t n -> p g (t n)")).then_inc(scr, 16)
                sp.wait_ge(scr, 16 * 17 * (b + 1))

            def load_s(n, par):
                sp.dma_start(sq_stk[par][:, :].bitcast(F), q_scr[bass.ds(n, 1), :, :]).then_inc(ld_s[par], 16)
                for r in range(REP):
                    sp.dma_start(sk_stk[par][32 * r:32 * (r + 1), r, :].bitcast(F),
                                 k_scr[bass.ds(n, 1), :, :]).then_inc(ld_s[par], 16)

            def load_t(n, par):
                for t in range(2):
                    for j in range(2):
                        r = 2 * t + j
                        sp.dma_start(tq_stk[par][t][64 * j:64 * j + 32, :].bitcast(F),
                                     q_scr[bass.ds(n, 1), 32 * r:32 * (r + 1), :]).then_inc(ld_t[par], 16)
                for j in range(2):
                    sp.dma_start(tk_stk[par][64 * j:64 * j + 32, :].bitcast(F),
                                 k_scr[bass.ds(n, 1), :, :]).then_inc(ld_t[par], 16)
                sp.dma_start(v_stk[par][:, :, :].rearrange("p t n -> p (t n)"),
                             v_scr[bass.ds(n, 1), :, :]).then_inc(ld_t[par], 16)

            def load_m(n, c, par):
                if c == 0:
                    sp.wait_ge(s_free, idx(n, T0) + 1)
                elif isinstance(n, int) and n == NG - 1:
                    sp.wait_ge(s_free, LAST_T1 + 1)
                else:
                    sp.wait_ge(s_free, NE * (n + 1) - 1 + T1 + 1)
                for r in range(REP):
                    j = r % 2
                    sp.dma_start(
                        tq_stk[par][r // 2][64 * j + 32:64 * j + 34, C2 * c:C2 * (c + 1)].bitcast(F)
                        .rearrange("p (i n) -> p i n", i=TC),
                        m_rows[c][8 * r:8 * (r + 1), :]).then_inc(ld_m[c][par], 16)

            def period(n, par, s_next=True, t_next=True, m_next=True):
                load_m(n, 1, par)
                if s_next:
                    sp.wait_ge(s_ready, NE * (n + 1) - 1)
                    load_s(n + 2, par)
                if t_next:
                    sp.wait_ge(pv_done, NS * n)
                    load_t(n + 1, 1 - par)
                if m_next:
                    load_m(n + 1, 0, 1 - par)

            sp.wait_ge(zeroed, 2)
            for par in range(2):
                load_s(par, par)
                load_t(par, par)
            load_m(0, 0, 0)
            period(0, 0, t_next=False)
            with sp.Fori(0, 2) as it:
                period(1 + 2 * it, 1)
                period(2 + 2 * it, 0)
            period(5, 1)
            period(6, 0, s_next=False)
            period(7, 1, s_next=False, t_next=False, m_next=False)

            with sp.Fori(0, B * NC_) as ch:
                sp.wait_ge(d_acc, E * TC * (ch + 1))
                sp.dma_start(out_v[bass.ds(TC * ch, TC), :, :].rearrange("t p d -> p t d"),
                             x[:, bass.ds(TC * ch, TC), :]).then_inc(st, 16)
            sp.wait_ge(st, 16 * B * NC_)

        @block.gpsimd
        def _(pool):
            pool.memset(ident[:, :], 0.0).then_inc(cst, 1)
            pool.memset(ident_bf[:, :], 0.0).then_inc(cst, 1)
            pool.memset(mask_bf[:, :], 0.0).then_inc(cst, 1)
            pool.memset(tri[:, :, :], 1.0).then_inc(cst, 1)
            pool.memset(eps_c[:, :], EPS).then_inc(cst, 1)
            pool.memset(tick[:, :], 0.0).then_inc(cst, 1)
            for i in range(2):
                pool.memset(sk_stk[i][:, :, :].bitcast(F), 0.0).then_inc(zeroed, 1)
            pool.wait_ge(cst, 6)
            for m in (ident, ident_bf):
                pool.affine_select(out=m[:, :], in_=m[:, :], compare_op=ALU.not_equal, fill=1.0,
                                   base=0, pattern=[[-1, P]], channel_multiplier=1).then_inc(cst, 1)
            pool.affine_select(out=mask_bf[:, :], in_=mask_bf[:, :], compare_op=ALU.is_ge, fill=MASKED,
                               base=0, pattern=[[-1, P]], channel_multiplier=1).then_inc(cst, 1)
            pool.affine_select(out=tri[:, :, :], in_=tri[:, :, :], compare_op=ALU.is_gt, fill=0.0,
                               base=0, pattern=[[1, E], [-1, E]], channel_multiplier=0).then_inc(cst, 1)
            pool.memset(vaug[:, :, :, HD:HD + 1], 1.0).then_inc(cst, 1)
            pool.memset(vaug[:, :, :, HD + 1:32], 0.0).then_inc(cst, 1)
            pool.wait_ge(w_hi, 1)
            pool.tensor_tensor(w2l[:, :, :, :], w2r[:, :, :, :], w2h[:, :, :, :].bitcast(F),
                               ALU.subtract).then_inc(w_lo, 1)
            for i in range(2):
                pool.wait_ge(w_hi, 2 + i)
                e0, e1 = i * E // 2, (i + 1) * E // 2
                pool.tensor_tensor(w13l[:, e0:e1, :], w13r[:, e0:e1, :],
                                   w13h[:, e0:e1, :].bitcast(F), ALU.subtract).then_inc(w_lo, 1)
            pool.wait_ge(scr, 16 * 17 * B)
            pool.wait_ge(w_lo, 3)
            for i in range(2):
                for j in range(2):
                    pool.wait_ge(cst, 12 + 2 * i + j)
                    pool.memset(tk_stk[i][64 * j + 32:64 * j + 34, :].bitcast(F), 1.0).then_inc(cst, 1)

            pool.wait_ge(cst, 16)

            def period(n):
                for s, (c, j) in enumerate(SLOTS):
                    if not DIAG[s]:
                        continue
                    for t in range(2):
                        v = 2 * s + t
                        if not (isinstance(n, int) and MASK_NO[s] + t == 0):
                            pool.wait_ge(k_done, NMASK * n + MASK_NO[s] + t)
                        pool.wait_ge(e_done, NU * n + v + 1)
                        blk = pt[:, v % NPB, :, 0:P]
                        pool.tensor_tensor(tick[:, 1:2], tick[:, 0:1], tick[:, 0:1], ALU.mult)
                        pool.affine_select(out=blk, in_=blk, compare_op=ALU.is_ge, fill=0.0, base=0,
                                           pattern=[[0, 2], [1, P]], channel_multiplier=-1).then_inc(k_done, 1)

            period(0)
            with pool.Fori(1, NG) as n:
                period(n)

            def chunk(ch, first=False):
                for m in range(2 * E):
                    pool.wait_ge(d_hi, 2 * E * ch + m + 1)
                    if not (first and m < 4):
                        pool.wait_ge(d_dn, E * ch + max(m // 2 - 1, 0))
                    pool.tensor_tensor(gl[m % 4][:, :], gg[m % 2][:, :], gh[m % 4][:, :].bitcast(F),
                                       ALU.subtract).then_inc(d_lo, 1)

            chunk(0, first=True)
            with pool.Fori(1, B * NC_) as ch:
                chunk(ch)

        @block.scalar
        def _(act):
            act.wait_ge(cst, 12)

            def root(b, n):
                act.wait_ge(a_var, n)
                act.activation(var_t[:, T * b:T * (b + 1)], var_t[:, T * b:T * (b + 1)], ACT.Sqrt,
                               bias=eps_c[:, 0:1]).then_inc(a_std, 1)

            def copy_t(b, dst, k, scale=None):
                for c in range(NC_):
                    act.wait_ge(a_tr, k + c + 1)
                    src = tr_bank(b, k, c)
                    if scale is None:
                        act.copy(dst[:, C2 * c:C2 * (c + 1)], src).then_inc(a_ht, 1)
                    else:
                        act.activation(dst[:, C2 * c:C2 * (c + 1)], src, ACT.Copy,
                                       scale=scale).then_inc(a_ht, 1)

            root(0, 1)
            root(1, 2)
            copy_t(0, ht_a[0], 0)
            copy_t(1, ht_a[1], 2)
            root(0, 3)
            root(0, 4)
            root(1, 5)
            root(1, 6)
            act.wait_ge(ld_moe, 32)
            act.copy(w2h[:, :, :, :], w2r[:, :, :, :]).then_inc(w_hi, 1)
            for i in range(2):
                e0, e1 = i * E // 2, (i + 1) * E // 2
                act.copy(w13h[:, e0:e1, :], w13r[:, e0:e1, :]).then_inc(w_hi, 1)
            act.wait_ge(ld_w, 16 * 6)
            copy_t(0, ht_a[0], 4, ln1c[:, 0:1])
            copy_t(1, ht_a[1], 6, ln1c[:, 0:1])

            for b in range(B):
                if b:
                    act.wait_ge(scr, 16 * 17)
                act.wait_ge(a_sum, 3 * b + 1)
                act.copy(k_hi[:, :], t_cos[0:64, :]).then_inc(a_hi, 1)
                act.wait_ge(a_sum, 3 * b + 2)
                act.copy(q_hi[:, 0:C2], t_cos[:, :]).then_inc(a_hi, 1)
                act.wait_ge(a_v, b + 1)
                act.copy(vaug[:, :, :, 0:HD].rearrange("p g t d -> p t g d"),
                         BK[4 * b + 2][:, 0:T * NKV * HD].rearrange("p (t g d) -> p t g d", t=T, g=NKV)
                         ).then_inc(a_vs, 1)
                act.wait_ge(a_sum, 3 * b + 3)
                act.copy(q_hi[:, C2:S], t_cos[:, :]).then_inc(a_hi, 1)

            act.wait_ge(scr, 16 * 17 * B)

            def o_copy(n, c):
                act.wait_ge(pv_done, NS * n + (TC if c == 0 else NS))
                if not (isinstance(n, int) and n == 0):
                    act.wait_ge(o_tr, 2 * n - 1 if c == 0 else 2 * n + 1)
                act.copy(o_sb[c][:, :], obank[c][:, :]).then_inc(o_cp, 1)

            def period(n, first=False):
                for v in range(NU):
                    c, j = SLOTS[v // 2]
                    w = slot_cols(c, j)[1]
                    act.wait_ge(t_done, NU * n + v + 1)
                    if not (first and v < NPB):
                        act.wait_ge(pv_done, NS * n + (v - NPB) // 2 + 1)
                    act.activation(pt[:, v % NPB, :, 0:w], pair[v % 2][:, :, 0:w], ACT.Exp).then_inc(e_done, 1)
                    if v == 2 * LAG + 1 and not first:
                        o_copy(n - 1, 1)
                    if v == 2 * (TC + LAG) + 1:
                        o_copy(n, 0)

            period(0, first=True)
            with act.Fori(1, NG) as n:
                period(n)
            o_copy(NG - 1, 1)

            for b in range(B):
                for c in range(NC_):
                    act.wait_ge(c_tr, 2 * b + c + 1)
                    act.copy(ot[b][:, C2 * c:C2 * (c + 1)], BK[4 * b + c]).then_inc(c_cp, 1)
            for b in range(B):
                act.wait_ge(c_x2, b + 1)
                for i in range(T):
                    last = act.activation(h2[:, T * b + i, :], y[:, T * b + i, :], ACT.Square,
                                          accum_out=rms[:, T * b + i:T * b + i + 1])
                    last.then_inc(c_sq, 1)
                act.wait_ge(c_sq, T * (b + 1))
                act.activation(rms[:, T * b:T * (b + 1)], rms[:, T * b:T * (b + 1)], ACT.Sqrt,
                               scale=1.0 / HID, bias=eps_c[:, 0:1]).then_inc(c_rt, 1)
            for b in range(B):
                for c in range(NC_):
                    act.wait_ge(c_tr, 2 * B + 2 * b + c + 1)
                    act.activation(h2t[:, S * b + C2 * c:S * b + C2 * (c + 1)], BK[4 * b + 2 + c], ACT.Copy,
                                   scale=ln2c[:, 0:1]).then_inc(c_cp, 1)
                act.wait_ge(c_cp, 2 * B + 2 * (b + 1))
                act.copy(h2h[:, S * b:S * (b + 1)], h2t[:, S * b:S * (b + 1)]).then_inc(c_hi, 1)
            for b in range(B):
                act.wait_ge(c_sh, b + 1)
                act.activation(ex[:, :, :], lg[:, :, :], ACT.Exp).then_inc(c_ex, 1)

            def chunk(ch, first=False):
                def hi_part(m):
                    act.wait_ge(d_g, 2 * E * ch + m + 1)
                    if not (first and m < 4):
                        act.wait_ge(d_dn, E * ch + max(m // 2 - 1, 0))
                    act.copy(gh[m % 4][:, :], gg[m % 2][:, :]).then_inc(d_hi, 1)

                for m in range(2 * E):
                    act.wait_ge(d_a, 2 * E * ch + m + 1)
                    if not (first and m < 2):
                        act.wait_ge(d_g, 2 * E * ch + max(m - 1, 0))
                    act.activation(silu[m % 2][:, :], bank[m % 2][:, :], ACT.Silu).then_inc(d_s, 1)
                    if m:
                        hi_part(m - 1)
                hi_part(2 * E - 1)

            chunk(0, first=True)
            with act.Fori(1, B * NC_) as ch:
                chunk(ch)

        @block.vector
        def _(dve):
            steps = [0]

            def link(ins):
                steps[0] += 1
                ins.then_inc(vq, 1)
                dve.wait_ge(vq, steps[0])

            def variance(b):
                for i in range(T * b, T * (b + 1)):
                    last = dve.bn_stats(stats[:, i, :], x[:, i, :])
                link(last)
                for i in range(T * b, T * (b + 1)):
                    last = dve.bn_aggr(mv[:, i, :], stats[:, i, :])
                link(last)

            def inverse_root(b, n):
                dve.wait_ge(a_std, n)
                link(dve.reciprocal(rstd[:, T * b:T * (b + 1)], var_t[:, T * b:T * (b + 1)]))

            bt = [slice(T * b, T * (b + 1)) for b in range(B)]
            for b in range(B):
                dve.wait_ge(ld_x[b], 16)
                variance(b)
                dve.tensor_copy(var_t[:, bt[b]], mv[:, bt[b], 1]).then_inc(a_var, 1)
            for b in range(B):
                inverse_root(b, b + 1)
                for i in range(T):
                    k = T * b + i
                    last = dve.tensor_scalar(h_a[b][:, i, :], x[:, k, :], mv[:, k, 0:1], rstd[:, k:k + 1],
                                             ALU.subtract, ALU.mult)
                last.then_inc(a_h, 1)
            for b in range(B):
                dve.wait_ge(a_g, b + 1)
                dve.tensor_copy(g_sb[b][:, :], BK[4 * b][:, 0:HID]).then_inc(a_gs, 1)
            for b in range(B):
                dve.wait_ge(a_m, b + 1)
                dve.tensor_copy(m_sb[b][:, :], BK[4 * b + 3][:, 0:HID]).then_inc(a_ms, 1)
            for b in range(B):
                for c in range(NC_):
                    dve.wait_ge(a_att, 2 * b + c + 1)
                    xs = x[:, T * b + TC * c:T * b + TC * (c + 1), :].rearrange("p t d -> p (t d)")
                    last = dve.tensor_tensor(xs, xs, BK[4 * b + c], ALU.add)
                    last.then_inc(a_x1, 1)
                dve.wait_ge(a_x1, 2 * (b + 1))
                variance(b)
                dve.tensor_copy(var_t[:, bt[b]], mv[:, bt[b], 1]).then_inc(a_var, 1)
                inverse_root(b, 3 + 2 * b)
                link(dve.tensor_tensor(rms[:, bt[b]], rstd[:, bt[b]], rstd[:, bt[b]], ALU.mult))
                dve.tensor_tensor(var_t[:, bt[b]], rms[:, bt[b]], mv[:, bt[b], 1], ALU.mult).then_inc(a_var, 1)
                for i in range(T):
                    k = T * b + i
                    last = dve.tensor_scalar(y[:, k, :], x[:, k, :], mv[:, k, 0:1], rstd[:, k:k + 1],
                                             ALU.subtract, ALU.mult)
                link(last)
                dve.wait_ge(a_std, 4 + 2 * b)
                link(dve.reciprocal(rms[:, bt[b]], var_t[:, bt[b]]))
                dve.wait_ge(a_ms, b + 1)
                for i in range(T):
                    k = T * b + i
                    last = dve.tensor_scalar(h_a[b][:, i, :], y[:, k, :], rms[:, k:k + 1], None, ALU.mult)
                last.then_inc(a_h, 1)

            dve.wait_ge(ld_rope, 64)

            def rotate(n, rows, direct, turned, cos, sin, hi, lo, b):
                dve.wait_ge(a_qk, n + 1)
                if n:
                    dve.wait_ge(a_hi, n)
                last = dve.tensor_tensor(t_cos[0:rows, :], direct, cos, ALU.mult)
                link(dve.tensor_tensor(t_sin[0:rows, :], turned, sin, ALU.mult))
                last = dve.tensor_tensor(t_cos[0:rows, :], t_cos[0:rows, :], t_sin[0:rows, :], ALU.add)
                last.then_inc(a_sum, 1)
                dve.wait_ge(a_hi, n + 1)
                dve.tensor_tensor(lo, t_cos[0:rows, :], hi.bitcast(F), ALU.subtract).then_inc(a_lo, 1)
                dve.wait_ge(a_lo, n + 1)

            for b in range(B):
                X = BK[4 * b:4 * b + 4]
                rotate(3 * b, 64, X[2][0:64, :], X[3][0:64, :], ck[:, :], sk[:, :],
                       k_hi[:, :], k_lo[:, :], b)
                for c in range(NC_):
                    cs = slice(C2 * c, C2 * (c + 1))
                    rotate(3 * b + 1 + c, P, X[0], X[1], cq[:, cs], sq[:, cs], q_hi[:, cs], q_lo[:, cs], b)

            dve.wait_ge(scr, 16 * 17 * B)

            def negate(n, c):
                src = mx[:, c, :, :].rearrange("p i h -> p h i")
                dve.tensor_scalar(neg[:, c, :, 0, :].bitcast(FR), src, -1.0, None, ALU.mult).then_inc(n_hi, 1)
                dve.wait_ge(n_hi, 2 * n + c + 1)
                dve.scalar_tensor_tensor(neg[:, c, :, 1, :].bitcast(FR), src, -1.0, neg[:, c, :, 0, :],
                                         ALU.mult, ALU.subtract).then_inc(m_neg, 1)

            def element(n, half, par, e, no, bk):
                kind, u = STREAM[e]
                dve.wait_ge(s_ready, no + 1)
                src = bank[bk]
                if kind == "s":
                    i, k0, nb, heads = u
                    w = nb * P
                    dst = mx[:, i // TC, i % TC, heads[0]:heads[-1] + 1] if k0 == 0 \
                        else mx2[:, i - TC, heads[0]:heads[-1] + 1]
                    dve.reduce_max(dst, src[:, 0:w * len(heads)].rearrange("p (h k) -> p h k", h=len(heads)),
                                   AX.X).then_inc(s_free, 1)
                    if UNIT_OF[e] == N_LOW - 1:
                        dve.wait_ge(s_free, no + 1)
                        negate(n, 0)
                    if e == NE - 1:
                        dve.wait_ge(s_free, no + 1)
                        dve.tensor_tensor(mx[:, 1, :, :], mx[:, 1, :, :], mx2[:, :, :], ALU.max).then_inc(n_mx, 1)
                        dve.wait_ge(n_mx, n + 1)
                        negate(n, 1)
                elif kind == "t0":
                    rows(n, half, par, 0, src)
                else:
                    rows(n - 1, half - (1 - par), 1 - par, 1, src)

            def rows(n, half, par, c, src):
                if not (isinstance(n, int) and n == 0):
                    dve.wait_ge(ld_m[c][1 - par], 64 * (half + par))
                dve.tensor_copy(m_rows[c][:, :], src[0:32, 0:P]).then_inc(s_free, 1)

            def o_norm(n, c):
                src = obank[c][:, :].rearrange("p (i h d) -> p i h d", i=TC, h=REP)
                dve.wait_ge(o_tr, 2 * n + c + 1)
                dve.reciprocal(o_rec[c][:, :, :], src[:, :, :, HD]).then_inc(n_rc, 1)
                dve.wait_ge(n_rc, 2 * n + c + 1)
                dst = otok[:, TC * c:TC * (c + 1), bass.ds(n, 1), :].rearrange("p i g (h d) -> p (i g) h d", h=REP)
                dve.tensor_tensor(dst, src[:, :, :, 0:HD],
                                  o_rec[c][:, :, :].unsqueeze(3).broadcast_to([P, TC, REP, HD]),
                                  ALU.mult).then_inc(o_nm, 1)

            def period(n, half, par, last=False, first=False):
                for s in range(NS):
                    if not last:
                        for e in IN_SLOT[s]:
                            element(n + 1, half + par, 1 - par, e, idx(n + 1, e), bank_no(n + 1, e))
                    elif s == 0:
                        element(NG, half + par, 1 - par, T1, LAST_T1, LAST_T1 % 2)
                    if s == TR1_SLOT and not first:
                        o_norm(n - 1, 1)
                    if s == TR0_SLOT:
                        o_norm(n, 0)

            for e in range(NE):
                if STREAM[e][0] != "t1":
                    element(0, 0, 0, e, idx(0, e), bank_no(0, e))
            period(0, 0, 0, first=True)
            with dve.Fori(0, 3) as it:
                period(1 + 2 * it, it, 1)
                period(2 + 2 * it, it + 1, 0)
            period(NG - 1, 3, 1, last=True)
            o_norm(NG - 1, 1)

            for b in range(B):
                for c in range(NC_):
                    dve.wait_ge(c_wo, 2 * b + c + 1)
                    ys = y[:, T * b + TC * c:T * b + TC * (c + 1), :].rearrange("p t d -> p (t d)")
                    last = dve.tensor_tensor(ys, ys, BK[4 * b + 2 + c], ALU.add)
                link(last)
                dve.tensor_tensor(x[:, bt[b], :], x[:, bt[b], :], y[:, bt[b], :], ALU.add).then_inc(c_x2, 1)
            for b in range(B):
                dve.wait_ge(c_rt, b + 1)
                link(dve.reciprocal(rms[:, bt[b]], rms[:, bt[b]]))
                for i in range(T):
                    k = T * b + i
                    last = dve.tensor_scalar(h2[:, k, :], y[:, k, :], rms[:, k:k + 1], None, ALU.mult)
                last.then_inc(c_h, 1)
            for b in range(B):
                bs = slice(S * b, S * (b + 1))
                dve.wait_ge(c_hi, b + 1)
                dve.tensor_tensor(h2l[:, bs], h2t[:, bs], h2h[:, bs].bitcast(F), ALU.subtract).then_inc(c_lo, 1)
            for b in range(B):
                dve.wait_ge(c_lg, b + 1)
                src = BK[4 * b][:, 0:T * E].rearrange("p (t e) -> p t e", t=T)
                link(dve.reduce_max(r8[:, 0, :], src, AX.X))
                dve.tensor_tensor(lg[:, :, :], src, r8[:, 0, :].unsqueeze(2).broadcast_to([P, T, E]),
                                  ALU.subtract).then_inc(c_sh, 1)
                dve.wait_ge(c_ex, b + 1)
                f_of = ex[:, :, :].unsqueeze(2).broadcast_to([P, T, E, E])
                e_of = ex[:, :, :].unsqueeze(3).broadcast_to([P, T, E, E])
                dve.tensor_tensor(cmp1[:, :, :, :], f_of, e_of, ALU.is_gt)
                link(dve.tensor_tensor(cmp2[:, :, :, :], f_of, e_of, ALU.is_equal))
                link(dve.tensor_tensor(cmp2[:, :, :, :], cmp2[:, :, :, :],
                                       tri[:, :, :].unsqueeze(1).broadcast_to([P, T, E, E]), ALU.mult))
                link(dve.tensor_tensor(cmp1[:, :, :, :], cmp1[:, :, :, :], cmp2[:, :, :, :], ALU.add))
                link(dve.reduce_sum(lg[:, :, :], cmp1[:, :, :, :], AX.X))
                link(dve.scalar_tensor_tensor(ex[:, :, :], lg[:, :, :], 1.5, ex[:, :, :], ALU.is_lt, ALU.mult))
                link(dve.reduce_sum(r8[:, 0, :], ex[:, :, :], AX.X))
                link(dve.reciprocal(r8[:, 1, :], r8[:, 0, :]))
                link(dve.tensor_tensor(gate_w[:, bt[b], :], ex[:, :, :],
                                       r8[:, 1, :].unsqueeze(2).broadcast_to([P, T, E]), ALU.mult))

            def chunk(ch, first=False):
                def add_up(e):
                    dve.wait_ge(d_dn, E * ch + e + 1)
                    if not (first and e == 0):
                        dve.wait_ge(d_acc, TC * (E * ch + e))
                    for i in range(TC):
                        xs = x[:, bass.ds(TC * ch + i, 1), :].rearrange("p t d -> p (t d)")
                        gs = gate_w[:, bass.ds(TC * ch + i, 1), e:e + 1].rearrange("p t d -> p (t d)")
                        dve.scalar_tensor_tensor(xs, obank[e % 2][:, P * i:P * (i + 1)], gs, xs,
                                                 ALU.mult, ALU.add).then_inc(d_acc, 1)

                for m in range(2 * E):
                    dve.wait_ge(d_s, 2 * E * ch + m + 1)
                    dve.wait_ge(d_u, 2 * E * ch + m + 1)
                    if not (first and m < 2):
                        dve.wait_ge(d_lo, 2 * E * ch + max(m - 1, 0))
                    dve.tensor_tensor(gg[m % 2][:, :], silu[m % 2][:, :], pair[m % 2][:, 0, :],
                                      ALU.mult).then_inc(d_g, 1)
                    if m >= 5 and m % 2 == 1:
                        add_up((m - 5) // 2)
                add_up(E - 2)
                add_up(E - 1)

            chunk(0, first=True)
            with dve.Fori(1, B * NC_) as ch:
                chunk(ch)

        @block.tensor
        def _(pe):
            pe.wait_ge(cst, 12)

            def transposes(b, k):
                for c in range(NC_):
                    for i in range(TC):
                        last = pe.transpose(tr_bank(b, k, c)[:, P * i:P * (i + 1)],
                                            h_a[b][:, TC * c + i, :], ident[:, :])
                    last.then_inc(a_tr, 1)

            for b in range(B):
                pe.wait_ge(a_h, b + 1)
                for i in range(T):
                    last = pe.matmul(BK[4 * b][:, 0:HID], h_a[b][:, i, :], h_a[b][:, i, :],
                                     start=i == 0, stop=i == T - 1)
                last.then_inc(a_g, 1)
                transposes(b, 2 * b)
            pe.wait_ge(ld_w, 16 * 6)
            for b in range(B):
                pe.wait_ge(a_gs, b + 1)
                pe.matmul(BK[4 * b + 3][:, 0:HID], qmat[:, :], g_sb[b][:, :], start=True,
                          stop=True).then_inc(a_m, 1)
            for b in range(B):
                pe.wait_ge(a_ms, b + 1)
                pe.wait_ge(a_ht, 2 * (b + 1))
                for c in range(NC_):
                    for i in range(TC):
                        t = TC * c + i
                        last = pe.matmul(BK[4 * b + c][:, P * i:P * (i + 1)], ht_a[b][:, P * t:P * (t + 1)],
                                         m_sb[b][:, :], start=True, stop=True)
                    last.then_inc(a_att, 1)
            for b in range(B):
                pe.wait_ge(a_h, B + b + 1)
                transposes(b, 2 * B + 2 * b)
            for b in range(B):
                X = BK[4 * b:4 * b + 4]
                pe.wait_ge(a_ht, 2 * B + 2 * (b + 1))
                for bk, w0 in ((X[2], K0), (X[3], RK0)):
                    for c in range(NC_):
                        last = pe.matmul(bk[32 * c:32 * (c + 1), :], wqk_sb[:, w0:w0 + 32],
                                         ht_a[b][:, C2 * c:C2 * (c + 1)], start=True, stop=True)
                last.then_inc(a_qk, 1)
                for c in range(NC_):
                    if c:
                        pe.wait_ge(a_sum, 3 * b + 2)
                    for bk, w0 in ((X[0], QK0), (X[1], RQ0)):
                        last = pe.matmul(bk, wqk_sb[:, w0:w0 + P], ht_a[b][:, C2 * c:C2 * (c + 1)],
                                         start=True, stop=True)
                    last.then_inc(a_qk, 1)
                    if c == 0:
                        pe.wait_ge(a_sum, 3 * b + 1)
                        for i in range(T):
                            last = pe.matmul(X[2][:, 32 * i:32 * (i + 1)], ht_a[b][:, P * i:P * (i + 1)],
                                             wqk_sb[:, V0:V0 + 32], start=True, stop=True)
                        last.then_inc(a_v, 1)

            pe.wait_ge(a_lo, 3 * B)
            pe.wait_ge(a_vs, B)

            def element(n, half, par, e, no, bk):
                kind, u = STREAM[e]
                bk = bank[bk]
                if not (isinstance(no, int) and no < 2):
                    pe.wait_ge(s_free, no - 1)
                if kind == "s":
                    i, k0, nb, heads = u
                    w = nb * P
                    if UNIT_OF[e] == 0:
                        pe.wait_ge(ld_s[par], 16 * 5 * (half + 1))
                    diag = k0 + nb - 1 == i
                    nh = len(heads)
                    o = bk[:, 0:w * nh].rearrange("p (h k) -> p h k", h=nh)
                    last = pe.matmul(o, sq_stk[par][:, P * i:P * (i + 1)],
                                     sk_stk[par][:, heads[0]:heads[0] + nh, P * k0:P * k0 + w],
                                     start=True, stop=not diag)
                    if diag:
                        last = pe.matmul(o[:, :, w - P:w], ident_bf[:, :],
                                         mask_bf[:, :].unsqueeze(1).broadcast_to([P, nh, P]),
                                         start=False, stop=True)
                    last.then_inc(s_ready, 1)
                else:
                    g, c = (n, 0) if kind == "t0" else (n - 1, 1)
                    pe.wait_ge(m_neg, 2 * g + c + 1)
                    pe.transpose(bk[0:32, 0:P], neg[:, c, :, :, :].rearrange("p h s i -> p (h s i)"),
                                 ident[:, :]).then_inc(s_ready, 1)

            def times_v(n, par, s):
                c, j = SLOTS[s]
                q0, w = slot_cols(c, j)
                if DIAG[s]:
                    pe.wait_ge(k_done, NMASK * n + MASK_NO[s] + 2)
                pe.wait_ge(e_done, NU * n + 2 * s + 2)
                for r in range(REP):
                    last = pe.matmul(obank[c][32 * r:32 * (r + 1), q0:C2], v_stk[par][:, j, :],
                                     pt[:, (2 * s + r // 2) % NPB, r % 2, 0:w],
                                     start=j == 0, stop=j == TC * (c + 1) - 1)
                last.then_inc(pv_done, 1)

            def o_transposes(n, c):
                pe.wait_ge(o_cp, 2 * n + c + 1)
                for i in range(TC):
                    last = pe.transpose(obank[c][:, P * i:P * (i + 1)], o_sb[c][:, P * i:P * (i + 1)],
                                        ident[:, :])
                last.then_inc(o_tr, 1)

            def period(n, half, par, first=False, last=False):
                for s, (c, j) in enumerate(SLOTS):
                    q0, w = slot_cols(c, j)
                    if s == 0:
                        pe.wait_ge(ld_t[par], 16 * 7 * (half + 1))
                    if j == 0:
                        pe.wait_ge(ld_m[c][par], 64 * (half + 1))
                    todo = [] if last else list(IN_SLOT[s])
                    for t in range(2):
                        v = 2 * s + t
                        if not (first and v < 2):
                            pe.wait_ge(e_done, NU * n + v - 1)
                        for jj in range(2):
                            ins = pe.matmul(pair[v % 2][:, jj, 0:w], tk_stk[par][64 * jj:64 * jj + 34, P * j:P * (j + 1)],
                                            tq_stk[par][t][64 * jj:64 * jj + 34, C2 * c + q0:C2 * (c + 1)],
                                            start=True, stop=True)
                        ins.then_inc(t_done, 1)
                        if t == 0:
                            for e in todo[:len(todo) // 2]:
                                element(n + 1, half + par, 1 - par, e, idx(n + 1, e), bank_no(n + 1, e))
                    if s >= LAG:
                        if s - LAG == 0 and not first:
                            pe.wait_ge(o_nm, 2 * n - 1)
                        if s - LAG == TC and not first:
                            pe.wait_ge(o_nm, 2 * n)
                        times_v(n, par, s - LAG)
                    elif not first:
                        times_v(n - 1, 1 - par, NS - LAG + s)
                    for e in todo[len(todo) // 2:]:
                        element(n + 1, half + par, 1 - par, e, idx(n + 1, e), bank_no(n + 1, e))
                    if last and s == 0:
                        element(NG, half + par, 1 - par, T1, LAST_T1, LAST_T1 % 2)
                    if s == TR1_SLOT and not first:
                        o_transposes(n - 1, 1)
                    if s == TR0_SLOT:
                        o_transposes(n, 0)

            for e in range(NE):
                if STREAM[e][0] != "t1":
                    element(0, 0, 0, e, idx(0, e), bank_no(0, e))
            pe.wait_ge(cst, 16)
            period(0, 0, 0, first=True)
            with pe.Fori(0, 3) as it:
                period(1 + 2 * it, it, 1)
                period(2 + 2 * it, it + 1, 0)
            period(NG - 1, 3, 1, last=True)
            for s in range(NS - LAG, NS):
                times_v(NG - 1, 1, s)
            o_transposes(NG - 1, 1)

            pe.wait_ge(o_nm, 2 * NG)
            for b in range(B):
                for c in range(NC_):
                    for i in range(TC):
                        src = otok[:, TC * c + i, NKV * b:NKV * (b + 1), :].rearrange("p g d -> p (g d)")
                        last = pe.transpose(BK[4 * b + c][:, P * i:P * (i + 1)], src, ident[:, :])
                    last.then_inc(c_tr, 1)
            for b in range(B):
                for c in range(NC_):
                    pe.wait_ge(c_cp, 2 * b + c + 1)
                    for i in range(TC):
                        t = TC * c + i
                        last = pe.matmul(BK[4 * b + 2 + c][:, P * i:P * (i + 1)], ot[b][:, P * t:P * (t + 1)],
                                         wo_sb[:, :], start=True, stop=True)
                    last.then_inc(c_wo, 1)
            for b in range(B):
                pe.wait_ge(c_h, b + 1)
                for c in range(NC_):
                    for i in range(TC):
                        last = pe.transpose(BK[4 * b + 2 + c][:, P * i:P * (i + 1)],
                                            h2[:, T * b + TC * c + i, :], ident[:, :])
                    last.then_inc(c_tr, 1)
            for b in range(B):
                pe.wait_ge(c_cp, 2 * B + 2 * (b + 1))
                for i in range(T):
                    last = pe.matmul(BK[4 * b][:, E * i:E * (i + 1)],
                                     h2t[:, S * b + P * i:S * b + P * (i + 1)], gate_sb[:, :],
                                     start=True, stop=True)
                last.then_inc(c_lg, 1)

            pe.wait_ge(w_lo, 3)
            pe.wait_ge(c_lo, B)
            pe.wait_ge(c_sh, B)
            def chunk(ch, first=False):
                def down(e):
                    pe.wait_ge(d_hi, 2 * E * ch + 2 * e + 2)
                    pe.wait_ge(d_lo, 2 * E * ch + 2 * e + 2)
                    if not (first and e < 2):
                        pe.wait_ge(d_acc, TC * (E * ch + max(e - 1, 0)))
                    for i in range(TC):
                        terms = [(a[(2 * e + f) % 4], w[:, e, f, :]) for f in range(2)
                                 for a, w in ((gh, w2h), (gh, w2l), (gl, w2h))]
                        for k, (a, w) in enumerate(terms):
                            last = pe.matmul(obank[e % 2][:, P * i:P * (i + 1)], a[:, P * i:P * (i + 1)], w,
                                             start=k == 0, stop=k == len(terms) - 1)
                    last.then_inc(d_dn, 1)

                for e in range(E):
                    for f in range(2):
                        m = 2 * e + f
                        for which, bk, free, ready in ((0, bank[m % 2][:, :], d_s, d_a),
                                                       (1, pair[m % 2][:, 0, :], d_g, d_u)):
                            if not (first and m < 2):
                                pe.wait_ge(free, 2 * E * ch + max(m - 1, 0))
                            col = which * FFN + f * P
                            for k, (w, h) in enumerate(((w13h, h2h), (w13h, h2l), (w13l, h2h))):
                                last = pe.matmul(bk, w[:, e, col:col + P], h[:, bass.ds(C2 * ch, C2)],
                                                 start=k == 0, stop=k == 2)
                            last.then_inc(ready, 1)
                    if e:
                        down(e - 1)
                down(E - 1)

            chunk(0, first=True)
            with pe.Fori(1, B * NC_) as ch:
                chunk(ch)

    return nc


_INS = ["L0_attn_hidden_states", "L0_attn_queries", "L0_ffn_ln1_w", "L0_ffn_ln2_w", "L0_ffn_wqkv",
        "L0_ffn_wo", "L0_ffn_gate_w", "L0_ffn_w13", "L0_ffn_w2"]


def _rope_tables():
    import numpy as np
    inv = (np.float32(1.0) / np.float32(10000.0) ** (np.arange(0, HD, 2, dtype=np.float32) / np.float32(HD)))
    ang = np.arange(S, dtype=np.float32)[:, None] * inv.astype(np.float32)[None, :]
    ang = np.concatenate([ang, ang], axis=1).T
    cos, sin = np.cos(ang).astype(np.float32), np.sin(ang).astype(np.float32)
    sin = sin * np.where(np.arange(HD) < HD // 2, -1.0, 1.0).astype(np.float32)[:, None]
    scale = np.float32(HD ** -0.5)
    cq, sq = np.tile(cos * scale, (NH, 1)), np.tile(sin * scale, (NH, 1))

    def halves(a):
        a = np.tile(a, (NKV, 1))
        return np.concatenate([a[:, C2 * c:C2 * (c + 1)] for c in range(NC_)], axis=0)
    return [np.ascontiguousarray(a, dtype=np.float32) for a in (cq, sq, halves(cos), halves(sin))]


def kernel(**inputs):
    import numpy as np
    import concourse.bacc as bacc
    from concourse.bass_utils import run_bass_kernel_spmd

    a = {k: np.asarray(inputs[k]) for k in _INS}
    turned = (np.arange(HD) + HD // 2) % HD
    w = a["L0_ffn_wqkv"].T
    nq, nk = NH * HD, NKV * HD
    wq, wk, wv = w[:, :nq], w[:, nq:nq + nk], w[:, nq + nk:]
    wrq = wq.reshape(HID, NH, HD)[:, :, turned].reshape(HID, nq)
    wrk = wk.reshape(HID, NKV, HD)[:, :, turned].reshape(HID, nk)
    arrays = {
        "x_in": a["L0_attn_hidden_states"],
        "queries": a["L0_attn_queries"],
        "ln1": a["L0_ffn_ln1_w"].reshape(HID, 1),
        "ln2": a["L0_ffn_ln2_w"].reshape(HID, 1),
        "wqk": np.concatenate([wq, wrq, wk, wrk, wv], axis=1),
        "wo_t": a["L0_ffn_wo"].T,
        "gate_t": a["L0_ffn_gate_w"].T,
        "w13_t": a["L0_ffn_w13"].transpose(0, 2, 1),
        "w2_t": a["L0_ffn_w2"].transpose(0, 2, 1),
    }
    for name, table in zip(("cos_q", "sin_q", "cos_k", "sin_k"), _rope_tables()):
        arrays[name] = table
    arrays = {k: np.ascontiguousarray(v) for k, v in arrays.items()}
    nc = bacc.Bacc("TRN2", target_bir_lowering=False, num_devices=1)
    args = [nc.dram_tensor(k, v.shape, mybir.dt.from_np(v.dtype), kind="ExternalInput").ap()
            for k, v in arrays.items()]
    args.append(nc.dram_tensor("result", (B, S, HID), mybir.dt.float32, kind="ExternalOutput").ap())
    build_program(nc, *args)
    r = run_bass_kernel_spmd(nc, [arrays], core_ids=[0])
    return r.results[0]["result"]
```

```python
import concourse.bass as bass
from concourse import mybir
from contextlib import ExitStack

P = 128
B, S, HID = 2, 1024, 128
NH, NKV, HD = 16, 4, 8
REP = NH // NKV
E, FFN = 8, 256
EPS = 1e-5
T = S // P
C2 = 512
NC_ = S // C2
TC = C2 // P
NG = B * NKV
QK0, RQ0, K0, RK0, V0 = 0, 128, 256, 288, 320
WQK = 352
MASKED = -3.0e38

S_UNITS = []
for _i in range(T):
    for _k0, _nb in ((0, min(_i + 1, TC)), (TC, _i + 1 - TC)):
        if _nb > 0:
            _per = TC // _nb if _nb < 3 else 1
            for _h in range(0, REP, _per):
                S_UNITS.append((_i, _k0, _nb, list(range(_h, _h + _per))))
N_LOW = sum(1 for u in S_UNITS if u[0] < TC)
STREAM = [("s", u) for u in S_UNITS]
for _pos, _what in ((2, ("t", 1)), (14, ("o", 1)), (N_LOW + 6, ("t", 0)), (32, ("o", 0))):
    STREAM.insert(_pos, _what)
NSB = 3
NE = len(STREAM)
assert NE % NSB == 0
T1, T0, O1, O0 = (STREAM.index(x) for x in (("t", 1), ("t", 0), ("o", 1), ("o", 0)))
UNIT_OF = [sum(1 for x in STREAM[:e] if x[0] == "s") for e in range(NE)]


def issued(n, e):
    if STREAM[e][0] == "s":
        return n < NG
    if e == T0:
        return n < NG
    return n >= {T1: 1, O0: 1, O1: 2}[e] and (n < NG + (2 if e == O1 else 1))


_ORDER = [(n, e) for n in range(NG + 2) for e in range(NE) if issued(n, e)]
TAIL = _ORDER.index((NG, T1))


def idx(n, e):
    return _ORDER.index((n, e)) if isinstance(n, int) else n * NE - 4 + e


def bank_no(n, e):
    if isinstance(n, int):
        return NSB - 1 if n >= NG else idx(n, e) % NSB
    return (e - 4) % NSB


assert all(idx(n, e) == n * NE - 4 + e for n in (2, 5, NG - 1) for e in range(NE))
SLOTS = [(c, j) for c in range(NC_) for j in range(TC * (c + 1))]
NS = len(SLOTS)
NU = 2 * NS
NPB = 6
LAG = 2


def slot_cols(c, j):
    q0 = max(0, (j - TC * c) * P)
    return q0, C2 - q0


DIAG = [j >= TC * c for c, j in SLOTS]
MASK_NO = [2 * sum(DIAG[:s]) for s in range(NS)]
NMASK = 2 * sum(DIAG)




def period_items():
    main = []
    for s, (c, j) in enumerate(SLOTS):
        w = slot_cols(c, j)[1] / C2
        main += [(0.45 * w, ("st", s, 0)), (0.45 * w, ("st", s, 1)),
                 (0.92 * slot_cols(*SLOTS[(s - LAG) % NS])[1] / C2, ("pv", s))]
    cols = [x[1][2] * len(x[1][3]) * P / C2 if x[0] == "s" else 0.3 if x[0] == "t" else 1.2 for x in STREAM]
    on_pe = [0.22 * c + (0.15 if x[0] == "s" else 0) for c, x in zip(cols, STREAM)]
    on_dve = [0.54 * c + 0.13 for c in cols]
    total, read = sum(m[0] for m in main), sum(on_dve)
    items, e, pe_t, dve_t, done, main_done = [], 0, 0.0, 0.0, [], 0.0
    for k, (cost, item) in enumerate(main):
        while e < NE and (e < NSB or done[e - NSB] + 0.1 <= pe_t) \
                and sum(on_dve[:e]) / read <= (main_done + 0.5 * cost) / total + 0.02:
            items.append(("e", e))
            pe_t += on_pe[e]
            dve_t = max(dve_t, pe_t + 0.1) + on_dve[e]
            done.append(dve_t)
            e += 1
        items.append(item)
        pe_t += cost
        main_done += cost
    return items + [("e", k) for k in range(e, NE)]


ITEMS = period_items()
LAGD = 3


def build_program(nc, x_in, queries, ln1, ln2, wqk, wo_t, gate_t, w13_t, w2_t,
                  cos_q, sin_q, cos_k, sin_k, out):
    F, FR, BF = mybir.dt.float32, mybir.dt.float32r, mybir.dt.bfloat16
    ALU, ACT, AX = mybir.AluOpType, mybir.ActivationFunctionType, mybir.AxisListType

    ctx = ExitStack()
    with ctx:
        def sb(name, shape, dt=F, scope=ctx):
            return scope.enter_context(nc.sbuf_tensor(name, shape, dt))

        def sem(name):
            return ctx.enter_context(nc.semaphore(name))

        q_scr = nc.dram_tensor("q_scr", [NG, P, S], F, kind="Internal").ap()
        k_scr = nc.dram_tensor("k_scr", [NG, 32, S], F, kind="Internal").ap()
        g_scr = nc.dram_tensor("g_scr", [E, B * S], F, kind="Internal").ap()
        v_scr = nc.dram_tensor("v_scr", [NG, P, T * 32], F, kind="Internal").ap()

        x = sb("x", [P, B * T, HID])
        y = sb("y", [P, B * T, HID])
        otok = sb("otok", [P, T, NG, 32])
        w13h, w13l = sb("w13h", [P, E, 2 * FFN], FR), sb("w13l", [P, E, 2 * FFN], FR)
        w2h, w2l = sb("w2h", [P, E, 2, HID], FR), sb("w2l", [P, E, 2, HID], FR)
        qmat = sb("qmat", [P, HID])
        ln1c, ln2c = sb("ln1c", [P, 1]), sb("ln2c", [P, 1])
        wqk_sb = sb("wqk_sb", [P, WQK])
        wo_sb = sb("wo_sb", [P, HID])
        gate_sb = sb("gate_sb", [P, E])
        ident = sb("ident", [P, P])
        ident_bf, mask_bf = sb("ident_bf", [P, P], BF), sb("mask_bf", [P, P], BF)
        tick = sb("tick", [P, 2])
        tri = sb("tri", [P, E, E])
        eps_c, m_half = sb("eps_c", [P, 1]), sb("m_half", [P, T])
        stats = sb("stats", [P, B * T, 6])
        mv = sb("mv", [P, B * T, 2])
        var_t, rstd = sb("var_t", [P, B * T]), sb("rstd", [P, B * T])
        rms = sb("rms", [P, B * T])
        gate_w = sb("gate_w", [P, B * T, E])
        mx = sb("mx", [P, NC_, TC, REP])
        mx2 = sb("mx2", [P, TC, REP])
        neg = sb("neg", [P, NC_, REP, 2, TC])
        m_rows = [sb(f"m_rows{c}", [32, P]) for c in range(NC_)]
        o_sb = [sb(f"o_sb{c}", [P, C2]) for c in range(NC_)]
        o_rec = [sb(f"o_rec{c}", [P, TC, REP]) for c in range(NC_)]

        s_ab = ExitStack()
        w13r, w2r = sb("w13r", [P, E, 2 * FFN], F, s_ab), sb("w2r", [P, E, 2, HID], F, s_ab)
        sk_stk = [sb(f"sk_stk{i}", [P, REP, S], FR, s_ab) for i in range(2)]

        s_a = ExitStack()
        h_a = [sb(f"h_a{b}", [P, T, HID], F, s_a) for b in range(B)]
        ht_a = [sb(f"ht_a{b}", [P, S], F, s_a) for b in range(B)]
        g_sb = [sb(f"g_sb{b}", [P, HID], F, s_a) for b in range(B)]
        m_sb = [sb(f"m_sb{b}", [P, HID], F, s_a) for b in range(B)]
        cq, sq = sb("cq", [P, S], F, s_a), sb("sq", [P, S], F, s_a)
        ck, sk = sb("ck", [64, C2], F, s_a), sb("sk", [64, C2], F, s_a)
        t_cos, t_sin = sb("t_cos", [P, C2], F, s_a), sb("t_sin", [P, C2], F, s_a)
        q_hi, q_lo = sb("q_hi", [P, S], FR, s_a), sb("q_lo", [P, S], FR, s_a)
        k_hi, k_lo = sb("k_hi", [64, C2], FR, s_a), sb("k_lo", [64, C2], FR, s_a)
        vaug = sb("vaug", [P, NKV, T, 32], F, s_a)
        s_a.close()
        s_b = ExitStack()
        sq_stk = [sb(f"sq_stk{i}", [P, S], FR, s_b) for i in range(2)]
        tq_stk = [[sb(f"tq_stk{i}{t}", [P, S], FR, s_b) for t in range(2)] for i in range(2)]
        tk_stk = [sb(f"tk_stk{i}", [P, S], FR, s_b) for i in range(2)]
        v_stk = [sb(f"v_stk{i}", [P, T, 32], F, s_b) for i in range(2)]
        pt = sb("pt", [P, NPB, 2, C2], F, s_b)
        s_b.close()
        s_ab.close()
        s_c = ExitStack()
        h2h, h2l = sb("h2h", [P, B * S], FR, s_c), sb("h2l", [P, B * S], FR, s_c)
        ot = [sb(f"ot{b}", [P, S], F, s_c) for b in range(B)]
        h2 = sb("h2", [P, B * T, HID], F, s_c)
        h2t = sb("h2t", [P, B * S], F, s_c)
        stats2, mv2 = sb("stats2", [P, T, 6], F, s_c), sb("mv2", [P, T, 2], F, s_c)
        lg, ex = sb("lg", [P, T, E], F, s_c), sb("ex", [P, T, E], F, s_c)
        cmp1, cmp2 = sb("cmp1", [P, T, E, E], F, s_c), sb("cmp2", [P, T, E, E], F, s_c)
        r8 = sb("r8", [P, 2, T], F, s_c)
        gate_wt = [sb(f"gate_wt{b}", [E, S], F, s_c) for b in range(B)]
        wbc = [sb(f"wbc{i}", [P, C2], F, s_c) for i in range(4)]
        silu = [sb(f"silu{i}", [P, C2], F, s_c) for i in range(2)]
        sw = [sb(f"sw{i}", [P, C2], F, s_c) for i in range(2)]
        gg = [sb(f"gg{i}", [P, C2], F, s_c) for i in range(2)]
        gh = [sb(f"gh{i}", [P, C2], FR, s_c) for i in range(4)]
        gl = [sb(f"gl{i}", [P, C2], FR, s_c) for i in range(4)]
        out_t = sb("out_t", [P, C2], F, s_c)
        s_c.close()

        bank = [ctx.enter_context(nc.psum_tensor(f"bank{i}", [P, C2], F)) for i in range(2)]
        pair = [ctx.enter_context(nc.psum_tensor(f"pair{i}", [P, 2, C2], F)) for i in range(2)]
        obank = [ctx.enter_context(nc.psum_tensor(f"obank{i}", [P, C2], F)) for i in range(2)]
        BK = [bank[0][:, :], bank[1][:, :], pair[0][:, 0, :], pair[0][:, 1, :],
              pair[1][:, 0, :], pair[1][:, 1, :], obank[0][:, :], obank[1][:, :]]

        ld_x = [sem(f"ld_x{b}") for b in range(B)]
        ld_w = sem("ld_w")
        ld_rope = sem("ld_rope")
        ld_moe = sem("ld_moe")
        cst = sem("cst")
        zeroed = sem("zeroed")
        vq = sem("vq")
        aq = sem("aq")
        a_var = sem("a_var")
        a_std = sem("a_std")
        a_h = sem("a_h")
        a_tr = sem("a_tr")
        a_ht = sem("a_ht")
        a_g, a_gs = sem("a_g"), sem("a_gs")
        a_m, a_ms = sem("a_m"), sem("a_ms")
        a_att, a_x1 = sem("a_att"), sem("a_x1")
        a_qk = sem("a_qk")
        a_rope = sem("a_rope")
        a_v, a_vs = sem("a_v"), sem("a_vs")
        a_sum = sem("a_sum")
        a_hi = sem("a_hi")
        a_lo = sem("a_lo")
        scr = sem("scr")
        w_hi, w_lo = sem("w_hi"), sem("w_lo")
        ld_s = [sem(f"ld_s{i}") for i in range(2)]
        ld_t = [sem(f"ld_t{i}") for i in range(2)]
        s_ready, s_free = sem("s_ready"), sem("s_free")
        m_neg = sem("m_neg")
        n_hi, n_mx = sem("n_hi"), sem("n_mx")
        n_rc = sem("n_rc")
        ld_m = [[sem(f"ld_m{c}{i}") for i in range(2)] for c in range(NC_)]
        t_done = sem("t_done")
        e_done = sem("e_done")
        k_done = sem("k_done")
        pv_done = sem("pv_done")
        o_cp = sem("o_cp")
        c_tr, c_cp = sem("c_tr"), sem("c_cp")
        c_wo, c_h = sem("c_wo"), sem("c_h")
        c_var, c_rms = sem("c_var"), sem("c_rms")
        c_lg = sem("c_lg")
        c_sh, c_ex = sem("c_sh"), sem("c_ex")
        c_hi, c_lo, c_w = sem("c_hi"), sem("c_lo"), sem("c_w")
        c_gt, c_gc = sem("c_gt"), sem("c_gc")
        cv = sem("cv")
        gw_st = sem("gw_st")
        ld_b = [sem(f"ld_b{i}") for i in range(4)]
        d_a, d_u = sem("d_a"), sem("d_u")
        d_s, d_sw, d_g = sem("d_s"), sem("d_sw"), sem("d_g")
        d_hi, d_lo = sem("d_hi"), sem("d_lo")
        d_dn = sem("d_dn")
        d_o, d_tr = sem("d_o"), sem("d_tr")
        d_acc = sem("d_acc")
        st = sem("st")
        block = ctx.enter_context(nc.Block())

        out_v = out.rearrange("b (t p) d -> (b t) p d", p=P)
        x_v = x_in.rearrange("b (t p) d -> b p t d", p=P)

        S_BANKS = [BK[0], BK[1], BK[7]]
        o_acc = obank[0]

        def tr_bank(b, k, c):
            return BK[4 * b + (1 if k < 4 else 2) + c]

        BANKS_C = [(BK[0], BK[1]), (BK[3], BK[5])]
        C_AT = {"act": (3, 11, 15, 4, 9, 12), "dve0": (2, 3, 4, 6, 7, 8, 10), "dve1": (5, 6, 7, 10, 11, 12, 15),
                "pe0": (1, 2, 5, 6, 9), "pe1": (3, 5, 9, 10, 14)}

        @block.sync
        def _(sp):
            sp.dma_start(x[:, 0:T, :], x_v[0]).then_inc(ld_x[0], 16)
            for dst, src in ((qmat[:, :], queries), (ln1c[:, :], ln1), (ln2c[:, :], ln2),
                             (wqk_sb[:, :], wqk), (wo_sb[:, :], wo_t), (gate_sb[:, :], gate_t)):
                sp.dma_start(dst, src).then_inc(ld_w, 16)
            sp.dma_start(x[:, T:2 * T, :], x_v[1]).then_inc(ld_x[1], 16)
            for dst, src in ((cq, cos_q), (sq, sin_q), (ck, cos_k), (sk, sin_k)):
                sp.dma_start(dst[:, :], src).then_inc(ld_rope, 16)
            sp.dma_start(w13r[:, :, :], w13_t.rearrange("e h f -> h e f")).then_inc(ld_moe, 16)
            sp.dma_start(w2r[:, :, :, :],
                         w2_t.rearrange("e (t p) h -> p e t h", p=P)).then_inc(ld_moe, 16)
            for b in range(B):
                sp.wait_ge(a_hi, 3 * b + 1)
                sp.wait_ge(a_lo, 3 * b + 1)
                for part, slots in ((k_hi, (0, 2)), (k_lo, (1, 3))):
                    for s in slots:
                        for c in range(NC_):
                            sp.dma_start(
                                k_scr[NKV * b:NKV * (b + 1), HD * s:HD * (s + 1), C2 * c:C2 * (c + 1)],
                                part[32 * c:32 * (c + 1), :].bitcast(F)).then_inc(scr, 16)
                for c in range(NC_):
                    sp.wait_ge(a_hi, 3 * b + 2 + c)
                    sp.wait_ge(a_lo, 3 * b + 2 + c)
                    qv = q_scr[NKV * b:NKV * (b + 1)].rearrange("g (h s d) n -> (g h) s d n", h=REP, s=4)
                    for part, slots in ((q_hi, (0, 1)), (q_lo, (2, 3))):
                        for s in slots:
                            sp.dma_start(qv[:, s, :, C2 * c:C2 * (c + 1)],
                                         part[:, C2 * c:C2 * (c + 1)].bitcast(F)).then_inc(scr, 16)
                sp.wait_ge(a_vs, b + 1)
                sp.dma_start(v_scr[NKV * b:NKV * (b + 1)].rearrange("g p n -> p g n"),
                             vaug[:, :, :, :].rearrange("p g t n -> p g (t n)")).then_inc(scr, 16)
                sp.wait_ge(scr, 16 * 17 * (b + 1))

            def load_s(n, par):
                sp.dma_start(sq_stk[par][:, :].bitcast(F), q_scr[bass.ds(n, 1), :, :]).then_inc(ld_s[par], 16)
                for r in range(REP):
                    sp.dma_start(sk_stk[par][32 * r:32 * (r + 1), r, :].bitcast(F),
                                 k_scr[bass.ds(n, 1), :, :]).then_inc(ld_s[par], 16)

            def load_t(n, par):
                for t in range(2):
                    for j in range(2):
                        r = 2 * t + j
                        sp.dma_start(tq_stk[par][t][64 * j:64 * j + 32, :].bitcast(F),
                                     q_scr[bass.ds(n, 1), 32 * r:32 * (r + 1), :]).then_inc(ld_t[par], 16)
                for j in range(2):
                    sp.dma_start(tk_stk[par][64 * j:64 * j + 32, :].bitcast(F),
                                 k_scr[bass.ds(n, 1), :, :]).then_inc(ld_t[par], 16)
                sp.dma_start(v_stk[par][:, :, :].rearrange("p t n -> p (t n)"),
                             v_scr[bass.ds(n, 1), :, :]).then_inc(ld_t[par], 16)

            def load_m(n, c, par):
                sp.wait_ge(s_free, idx(n, T0) + 1 if c == 0 else idx(n + 1, T1) + 1)
                for r in range(REP):
                    j = r % 2
                    sp.dma_start(
                        tq_stk[par][r // 2][64 * j + 32:64 * j + 34, C2 * c:C2 * (c + 1)].bitcast(F)
                        .rearrange("p (i n) -> p i n", i=TC),
                        m_rows[c][8 * r:8 * (r + 1), :]).then_inc(ld_m[c][par], 16)

            def period(n, par, s_next=True, t_next=True, m_next=True):
                load_m(n, 1, par)
                if s_next:
                    sp.wait_ge(s_ready, idx(n, NE - 1) + 1)
                    load_s(n + 2, par)
                if t_next:
                    sp.wait_ge(pv_done, NS * n)
                    load_t(n + 1, 1 - par)
                if m_next:
                    load_m(n + 1, 0, 1 - par)

            sp.wait_ge(zeroed, 2)
            for par in range(2):
                load_s(par, par)
                load_t(par, par)
            load_m(0, 0, 0)
            period(0, 0, t_next=False)
            with sp.Fori(0, 2) as it:
                period(1 + 2 * it, 1)
                period(2 + 2 * it, 0)
            period(5, 1)
            period(6, 0, s_next=False)
            period(7, 1, s_next=False, t_next=False, m_next=False)

            def gate_store(b):
                sp.wait_ge(c_gc, 2 * (b + 1))
                sp.dma_start(g_scr[:, S * b:S * (b + 1)], gate_wt[b][:, :]).then_inc(gw_st, 16)
                sp.wait_ge(gw_st, 16 * (b + 1))

            def chunk(ch, first=False):
                for e in range(E):
                    if not (first and e < 4):
                        sp.wait_ge(d_sw, 2 * E * ch + 2 * (e - 4) + 2)
                    sp.dma_start(wbc[e % 4][:, :], g_scr[e:e + 1, bass.ds(C2 * ch, C2)]
                                 .broadcast_to([P, C2])).then_inc(ld_b[e % 4], 16)
                    if e == 5 and not first:
                        result(ch - 1)

            def result(ch):
                sp.wait_ge(d_acc, ch + 1)
                sp.dma_start(out_v[bass.ds(TC * ch, TC), :, :].rearrange("t p d -> p t d"),
                             x[:, bass.ds(TC * ch, TC), :]).then_inc(st, 16)

            gate_store(0)
            sp.wait_ge(pv_done, NS * NG)
            chunk(0, first=True)
            chunk(1)
            gate_store(1)
            with sp.Fori(2, B * NC_) as ch:
                chunk(ch)
            result(B * NC_ - 1)
            sp.wait_ge(st, 16 * B * NC_)

        @block.gpsimd
        def _(pool):
            pool.memset(ident[:, :], 0.0).then_inc(cst, 1)
            pool.memset(ident_bf[:, :], 0.0).then_inc(cst, 1)
            pool.memset(mask_bf[:, :], 0.0).then_inc(cst, 1)
            pool.memset(tri[:, :, :], 1.0).then_inc(cst, 1)
            pool.memset(eps_c[:, :], EPS).then_inc(cst, 1)
            pool.memset(tick[:, :], 0.0).then_inc(cst, 1)
            pool.memset(m_half[:, :], -0.5)
            for i in range(2):
                pool.memset(sk_stk[i][:, :, :].bitcast(F), 0.0).then_inc(zeroed, 1)
            pool.wait_ge(cst, 6)
            for m in (ident, ident_bf):
                pool.affine_select(out=m[:, :], in_=m[:, :], compare_op=ALU.not_equal, fill=1.0,
                                   base=0, pattern=[[-1, P]], channel_multiplier=1).then_inc(cst, 1)
            pool.affine_select(out=mask_bf[:, :], in_=mask_bf[:, :], compare_op=ALU.is_ge, fill=MASKED,
                               base=0, pattern=[[-1, P]], channel_multiplier=1).then_inc(cst, 1)
            pool.affine_select(out=tri[:, :, :], in_=tri[:, :, :], compare_op=ALU.is_gt, fill=0.0,
                               base=0, pattern=[[1, E], [-1, E]], channel_multiplier=0).then_inc(cst, 1)
            pool.memset(vaug[:, :, :, HD:HD + 1], 1.0).then_inc(cst, 1)
            pool.memset(vaug[:, :, :, HD + 1:32], 0.0).then_inc(cst, 1)
            pool.wait_ge(w_hi, 1)
            pool.tensor_tensor(w2l[:, :, :, :], w2r[:, :, :, :], w2h[:, :, :, :].bitcast(F),
                               ALU.subtract).then_inc(w_lo, 1)
            for i in range(2):
                pool.wait_ge(w_hi, 2 + i)
                e0, e1 = i * E // 2, (i + 1) * E // 2
                pool.tensor_tensor(w13l[:, e0:e1, :], w13r[:, e0:e1, :],
                                   w13h[:, e0:e1, :].bitcast(F), ALU.subtract).then_inc(w_lo, 1)
            pool.wait_ge(scr, 16 * 17 * B)
            pool.wait_ge(w_lo, 3)
            for i in range(2):
                for j in range(2):
                    pool.wait_ge(cst, 12 + 2 * i + j)
                    pool.memset(tk_stk[i][64 * j + 32:64 * j + 34, :].bitcast(F), 1.0).then_inc(cst, 1)

            pool.wait_ge(cst, 16)

            def period(n, last=False):
                for s, (c, j) in enumerate(SLOTS):
                    if not DIAG[s]:
                        continue
                    for t in range(2):
                        v = 2 * s + t
                        if not (isinstance(n, int) and n + MASK_NO[s] + t == 0):
                            pool.wait_ge(k_done, NMASK * n + MASK_NO[s] + t)
                        pool.wait_ge(e_done, NU * n + v + 1)
                        blk = pt[:, v % NPB, :, 0:P]
                        pool.tensor_tensor(tick[:, 1:2], tick[:, 0:1], tick[:, 0:1], ALU.mult)
                        pool.affine_select(out=blk, in_=blk, compare_op=ALU.is_ge, fill=0.0, base=0,
                                           pattern=[[0, 2], [1, P]], channel_multiplier=-1).then_inc(k_done, 1)
                        if last and v == 2 * C_AT["dve0"][1] + 1:
                            c_root(0)

            def c_root(b):
                pool.wait_ge(c_var, b + 1)
                r = rms[:, T * b:T * (b + 1)]
                pool.tensor_tensor(r, r, m_half[:, :], ALU.pow).then_inc(c_rms, 1)

            period(0)
            with pool.Fori(1, NG - 1) as n:
                period(n)
            period(NG - 1, last=True)

            def chunk(ch, first=False):
                for m in range(2 * E):
                    pool.wait_ge(d_hi, 2 * E * ch + m + 1)
                    if not (first and m < 4):
                        pool.wait_ge(d_dn, 2 * E * ch + m - 3)
                    pool.tensor_tensor(gl[m % 4][:, :], gg[m % 2][:, :], gh[m % 4][:, :].bitcast(F),
                                       ALU.subtract).then_inc(d_lo, 1)
                    if first and m == C_AT["dve1"][1]:
                        c_root(1)

            chunk(0, first=True)
            with pool.Fori(1, B * NC_) as ch:
                chunk(ch)

        @block.scalar
        def _(act):
            act.wait_ge(cst, 12)

            def root(b, n):
                act.wait_ge(a_var, n)
                act.activation(var_t[:, T * b:T * (b + 1)], var_t[:, T * b:T * (b + 1)], ACT.Sqrt,
                               bias=eps_c[:, 0:1]).then_inc(a_std, 1)

            def copy_t(b, dst, k, scale=None):
                for c in range(NC_):
                    act.wait_ge(a_tr, k + c + 1)
                    src = tr_bank(b, k, c)
                    if scale is None:
                        act.copy(dst[:, C2 * c:C2 * (c + 1)], src).then_inc(a_ht, 1)
                    else:
                        act.activation(dst[:, C2 * c:C2 * (c + 1)], src, ACT.Copy,
                                       scale=scale).then_inc(a_ht, 1)

            root(0, 1)
            root(1, 2)
            copy_t(0, ht_a[0], 0)
            copy_t(1, ht_a[1], 2)
            root(0, 3)
            root(0, 4)
            root(1, 5)
            root(1, 6)
            act.wait_ge(ld_moe, 32)
            act.copy(w2h[:, :, :, :], w2r[:, :, :, :]).then_inc(w_hi, 1)
            for i in range(2):
                e0, e1 = i * E // 2, (i + 1) * E // 2
                act.copy(w13h[:, e0:e1, :], w13r[:, e0:e1, :]).then_inc(w_hi, 1)
            act.wait_ge(ld_w, 16 * 6)
            copy_t(0, ht_a[0], 4, ln1c[:, 0:1])
            copy_t(1, ht_a[1], 6, ln1c[:, 0:1])

            for b in range(B):
                if b:
                    act.wait_ge(scr, 16 * 17)
                act.wait_ge(a_sum, 3 * b + 1)
                act.copy(k_hi[:, :], t_cos[0:64, :]).then_inc(a_hi, 1)
                act.wait_ge(a_sum, 3 * b + 2)
                act.copy(q_hi[:, 0:C2], t_cos[:, :]).then_inc(a_hi, 1)
                act.wait_ge(a_v, b + 1)
                act.copy(vaug[:, :, :, 0:HD].rearrange("p g t d -> p t g d"),
                         BK[4 * b + 2][:, 0:T * NKV * HD].rearrange("p (t g d) -> p t g d", t=T, g=NKV)
                         ).then_inc(a_vs, 1)
                act.wait_ge(a_sum, 3 * b + 3)
                act.copy(q_hi[:, C2:S], t_cos[:, :]).then_inc(a_hi, 1)

            act.wait_ge(scr, 16 * 17 * B)

            def o_copy(n, c):
                act.wait_ge(pv_done, NS * n + (TC if c == 0 else NS))
                if not (isinstance(n, int) and n == 0):
                    act.wait_ge(s_ready, idx(n, O0) + 1 if c == 0 else idx(n + 1, O1) + 1)
                act.copy(o_sb[c][:, :], o_acc[:, :]).then_inc(o_cp, 1)

            def c_ot(b, X):
                for c in range(NC_):
                    act.wait_ge(c_tr, 4 * b + c + 1)
                    act.copy(ot[b][:, C2 * c:C2 * (c + 1)], X[c]).then_inc(c_cp, 1)

            def c_h2t(b, X):
                for c in range(NC_):
                    cs = slice(S * b + C2 * c, S * b + C2 * (c + 1))
                    act.wait_ge(c_tr, 4 * b + 2 + c + 1)
                    act.activation(h2t[:, cs], X[c], ACT.Copy, scale=ln2c[:, 0:1]).then_inc(c_cp, 1)
                    act.activation(h2h[:, cs], X[c], ACT.Copy, scale=ln2c[:, 0:1]).then_inc(c_hi, 1)

            def c_exp(b, X):
                act.wait_ge(c_sh, b + 1)
                act.activation(ex[:, :, :], lg[:, :, :], ACT.Exp).then_inc(c_ex, 1)

            def period(n, first=False, extra={}):
                for v in range(NU):
                    c, j = SLOTS[v // 2]
                    w = slot_cols(c, j)[1]
                    act.wait_ge(t_done, NU * n + v + 1)
                    if not (first and v < NPB):
                        act.wait_ge(pv_done, NS * n + (v - NPB) // 2 + 1)
                    act.activation(pt[:, v % NPB, :, 0:w], pair[v % 2][:, :, 0:w], ACT.Exp).then_inc(e_done, 1)
                    if v == 2 * LAG - 1 and not first:
                        o_copy(n - 1, 1)
                    if v == 2 * (TC + LAG) - 1:
                        o_copy(n, 0)
                    if v in extra:
                        extra[v](0, BANKS_C[0])

            period(0, first=True)
            with act.Fori(1, NG - 1) as n:
                period(n)
            period(NG - 1, extra={C_AT["act"][0]: c_ot, C_AT["act"][1]: c_h2t, C_AT["act"][2]: c_exp})
            o_copy(NG - 1, 1)

            def finish():
                act.copy(out_t[:, :], obank[0][:, :]).then_inc(d_o, 1)

            def hi_part(ch, m, first):
                act.wait_ge(d_g, 2 * E * ch + m + 1)
                if not (first and m < 4):
                    act.wait_ge(d_dn, 2 * E * ch + m - 3)
                act.copy(gh[m % 4][:, :], gg[m % 2][:, :]).then_inc(d_hi, 1)

            def chunk(ch, first=False, extra={}):
                for m in range(2 * E):
                    if m == LAGD and not first:
                        act.wait_ge(d_dn, 2 * E * ch)
                        finish()
                    act.wait_ge(d_a, 2 * E * ch + m + 1)
                    if not (first and m < 2):
                        act.wait_ge(d_sw, 2 * E * ch + m - 1)
                    act.activation(silu[m % 2][:, :], bank[m % 2][:, :], ACT.Silu).then_inc(d_s, 1)
                    if m:
                        hi_part(ch, m - 1, first)
                    if m in extra:
                        extra[m](1, BANKS_C[1])
                hi_part(ch, 2 * E - 1, False)

            chunk(0, first=True, extra={C_AT["act"][3]: c_ot, C_AT["act"][4]: c_h2t, C_AT["act"][5]: c_exp})
            with act.Fori(1, B * NC_) as ch:
                chunk(ch)
            act.wait_ge(d_dn, 2 * E * B * NC_)
            finish()

        @block.vector
        def _(dve):
            steps = [0]

            def link(ins):
                steps[0] += 1
                ins.then_inc(vq, 1)
                dve.wait_ge(vq, steps[0])

            def variance(b):
                for i in range(T * b, T * (b + 1)):
                    last = dve.bn_stats(stats[:, i, :], x[:, i, :])
                link(last)
                for i in range(T * b, T * (b + 1)):
                    last = dve.bn_aggr(mv[:, i, :], stats[:, i, :])
                link(last)

            def inverse_root(b, n):
                dve.wait_ge(a_std, n)
                link(dve.reciprocal(rstd[:, T * b:T * (b + 1)], var_t[:, T * b:T * (b + 1)]))

            bt = [slice(T * b, T * (b + 1)) for b in range(B)]
            for b in range(B):
                dve.wait_ge(ld_x[b], 16)
                variance(b)
                dve.tensor_copy(var_t[:, bt[b]], mv[:, bt[b], 1]).then_inc(a_var, 1)
            for b in range(B):
                inverse_root(b, b + 1)
                for i in range(T):
                    k = T * b + i
                    last = dve.tensor_scalar(h_a[b][:, i, :], x[:, k, :], mv[:, k, 0:1], rstd[:, k:k + 1],
                                             ALU.subtract, ALU.mult)
                last.then_inc(a_h, 1)
            for b in range(B):
                dve.wait_ge(a_g, b + 1)
                dve.tensor_copy(g_sb[b][:, :], BK[4 * b][:, 0:HID]).then_inc(a_gs, 1)
            for b in range(B):
                dve.wait_ge(a_m, b + 1)
                dve.tensor_copy(m_sb[b][:, :], BK[4 * b + 3][:, 0:HID]).then_inc(a_ms, 1)
            for b in range(B):
                for c in range(NC_):
                    dve.wait_ge(a_att, 2 * b + c + 1)
                    xs = x[:, T * b + TC * c:T * b + TC * (c + 1), :].rearrange("p t d -> p (t d)")
                    last = dve.tensor_tensor(xs, xs, BK[4 * b + c], ALU.add)
                    last.then_inc(a_x1, 1)
                dve.wait_ge(a_x1, 2 * (b + 1))
                variance(b)
                dve.tensor_copy(var_t[:, bt[b]], mv[:, bt[b], 1]).then_inc(a_var, 1)
                inverse_root(b, 3 + 2 * b)
                link(dve.tensor_tensor(rms[:, bt[b]], rstd[:, bt[b]], rstd[:, bt[b]], ALU.mult))
                dve.tensor_tensor(var_t[:, bt[b]], rms[:, bt[b]], mv[:, bt[b], 1], ALU.mult).then_inc(a_var, 1)
                for i in range(T):
                    k = T * b + i
                    last = dve.tensor_scalar(y[:, k, :], x[:, k, :], mv[:, k, 0:1], rstd[:, k:k + 1],
                                             ALU.subtract, ALU.mult)
                link(last)
                dve.wait_ge(a_std, 4 + 2 * b)
                link(dve.reciprocal(rms[:, bt[b]], var_t[:, bt[b]]))
                dve.wait_ge(a_ms, b + 1)
                for i in range(T):
                    k = T * b + i
                    last = dve.tensor_scalar(h_a[b][:, i, :], y[:, k, :], rms[:, k:k + 1], None, ALU.mult)
                last.then_inc(a_h, 1)

            dve.wait_ge(ld_rope, 64)

            def rotate(n, rows, direct, turned, cos, sin, hi, lo, b):
                dve.wait_ge(a_qk, n + 1)
                if n:
                    dve.wait_ge(a_hi, n)
                last = dve.tensor_tensor(t_cos[0:rows, :], direct, cos, ALU.mult)
                link(dve.tensor_tensor(t_sin[0:rows, :], turned, sin, ALU.mult))
                last = dve.tensor_tensor(t_cos[0:rows, :], t_cos[0:rows, :], t_sin[0:rows, :], ALU.add)
                last.then_inc(a_sum, 1)
                dve.wait_ge(a_hi, n + 1)
                dve.tensor_tensor(lo, t_cos[0:rows, :], hi.bitcast(F), ALU.subtract).then_inc(a_lo, 1)
                dve.wait_ge(a_lo, n + 1)

            for b in range(B):
                X = BK[4 * b:4 * b + 4]
                rotate(3 * b, 64, X[2][0:64, :], X[3][0:64, :], ck[:, :], sk[:, :],
                       k_hi[:, :], k_lo[:, :], b)
                for c in range(NC_):
                    cs = slice(C2 * c, C2 * (c + 1))
                    rotate(3 * b + 1 + c, P, X[0], X[1], cq[:, cs], sq[:, cs], q_hi[:, cs], q_lo[:, cs], b)

            dve.wait_ge(scr, 16 * 17 * B)

            def negate(n, c):
                src = mx[:, c, :, :].rearrange("p i h -> p h i")
                dve.tensor_scalar(neg[:, c, :, 0, :].bitcast(FR), src, -1.0, None, ALU.mult).then_inc(n_hi, 1)
                dve.wait_ge(n_hi, 2 * n + c + 1)
                dve.scalar_tensor_tensor(neg[:, c, :, 1, :].bitcast(FR), src, -1.0, neg[:, c, :, 0, :],
                                         ALU.mult, ALU.subtract).then_inc(m_neg, 1)

            def element(n, half, par, e, no, bk):
                kind, u = STREAM[e]
                dve.wait_ge(s_ready, no + 1)
                src = S_BANKS[bk]
                if kind == "s":
                    i, k0, nb, heads = u
                    w = nb * P
                    dst = mx[:, i // TC, i % TC, heads[0]:heads[-1] + 1] if k0 == 0 \
                        else mx2[:, i - TC, heads[0]:heads[-1] + 1]
                    dve.reduce_max(dst, src[:, 0:w * len(heads)].rearrange("p (h k) -> p h k", h=len(heads)),
                                   AX.X).then_inc(s_free, 1)
                    if UNIT_OF[e] == N_LOW - 1:
                        dve.wait_ge(s_free, no + 1)
                        negate(n, 0)
                    if e == NE - 1:
                        dve.wait_ge(s_free, no + 1)
                        dve.tensor_tensor(mx[:, 1, :, :], mx[:, 1, :, :], mx2[:, :, :], ALU.max).then_inc(n_mx, 1)
                        dve.wait_ge(n_mx, n + 1)
                        negate(n, 1)
                elif e == T0:
                    rows(n, half, par, 0, src)
                elif e == T1:
                    rows(n - 1, half - (1 - par), 1 - par, 1, src)
                else:
                    o_norm(n - 1 if e == O0 else n - 2, 0 if e == O0 else 1, src)

            def rows(n, half, par, c, src):
                if not (isinstance(n, int) and n == 0):
                    dve.wait_ge(ld_m[c][1 - par], 64 * (half + par))
                dve.tensor_copy(m_rows[c][:, :], src[0:32, 0:P]).then_inc(s_free, 1)

            def o_norm(n, c, bk):
                src = bk.rearrange("p (i h d) -> p i h d", i=TC, h=REP)
                dve.reciprocal(o_rec[c][:, :, :], src[:, :, :, HD]).then_inc(n_rc, 1)
                dve.wait_ge(n_rc, 2 * n + c + 1)
                dst = otok[:, TC * c:TC * (c + 1), bass.ds(n, 1), :].rearrange("p i g (h d) -> p (i g) h d", h=REP)
                dve.tensor_tensor(dst, src[:, :, :, 0:HD],
                                  o_rec[c][:, :, :].unsqueeze(3).broadcast_to([P, TC, REP, HD]),
                                  ALU.mult).then_inc(s_free, 1)

            c_steps = [0]

            def c_link(ins):
                c_steps[0] += 1
                ins.then_inc(cv, 1)
                dve.wait_ge(cv, c_steps[0])

            def c_x2(b, X):
                for c in range(NC_):
                    dve.wait_ge(c_wo, 2 * b + c + 1)
                    ys = y[:, T * b + TC * c:T * b + TC * (c + 1), :].rearrange("p t d -> p (t d)")
                    last = dve.tensor_tensor(ys, ys, X[c], ALU.add)
                c_link(last)

            def c_stats(b, X):
                for i in range(T):
                    last = dve.bn_stats(stats2[:, i, :], y[:, T * b + i, :])
                c_link(last)
                for i in range(T):
                    last = dve.bn_aggr(mv2[:, i, :], stats2[:, i, :])
                c_link(last)
                r = rms[:, bt[b]]
                c_link(dve.tensor_tensor(r, mv2[:, :, 0], mv2[:, :, 0], ALU.mult))
                dve.scalar_tensor_tensor(r, mv2[:, :, 1], EPS, r, ALU.add, ALU.add).then_inc(c_var, 1)

            def c_norm(b, X):
                dve.wait_ge(c_rms, b + 1)
                for i in range(T):
                    k = T * b + i
                    last = dve.tensor_scalar(h2[:, k, :], y[:, k, :], rms[:, k:k + 1], None, ALU.mult)
                last.then_inc(c_h, 1)
                dve.tensor_tensor(x[:, bt[b], :], x[:, bt[b], :], y[:, bt[b], :], ALU.add)

            def c_lo_part(b, X):
                bs = slice(S * b, S * (b + 1))
                dve.wait_ge(c_hi, 2 * (b + 1))
                dve.tensor_tensor(h2l[:, bs], h2t[:, bs], h2h[:, bs].bitcast(F), ALU.subtract).then_inc(c_lo, 1)

            def c_shift(b, X):
                dve.wait_ge(c_lg, b + 1)
                src = X[0][:, 0:T * E].rearrange("p (t e) -> p t e", t=T)
                c_link(dve.reduce_max(r8[:, 0, :], src, AX.X))
                dve.tensor_tensor(lg[:, :, :], src, r8[:, 0, :].unsqueeze(2).broadcast_to([P, T, E]),
                                  ALU.subtract).then_inc(c_sh, 1)

            def c_top2(b, X):
                dve.wait_ge(c_ex, b + 1)
                f_of = ex[:, :, :].unsqueeze(2).broadcast_to([P, T, E, E])
                e_of = ex[:, :, :].unsqueeze(3).broadcast_to([P, T, E, E])
                dve.tensor_tensor(cmp1[:, :, :, :], f_of, e_of, ALU.is_gt)
                c_link(dve.tensor_tensor(cmp2[:, :, :, :], f_of, e_of, ALU.is_equal))
                c_link(dve.tensor_tensor(cmp2[:, :, :, :], cmp2[:, :, :, :],
                                         tri[:, :, :].unsqueeze(1).broadcast_to([P, T, E, E]), ALU.mult))
                c_link(dve.tensor_tensor(cmp1[:, :, :, :], cmp1[:, :, :, :], cmp2[:, :, :, :], ALU.add))
                c_link(dve.reduce_sum(lg[:, :, :], cmp1[:, :, :, :], AX.X))
                c_link(dve.scalar_tensor_tensor(ex[:, :, :], lg[:, :, :], 1.5, ex[:, :, :], ALU.is_lt, ALU.mult))
                c_link(dve.reduce_sum(r8[:, 0, :], ex[:, :, :], AX.X))
                c_link(dve.reciprocal(r8[:, 1, :], r8[:, 0, :]))
                dve.tensor_tensor(gate_w[:, bt[b], :], ex[:, :, :],
                                  r8[:, 1, :].unsqueeze(2).broadcast_to([P, T, E]), ALU.mult).then_inc(c_w, 1)

            def c_gate_rows(b, X):
                for c in range(NC_):
                    dve.wait_ge(c_gt, 2 * b + c + 1)
                    dve.tensor_copy(gate_wt[b][:, C2 * c:C2 * (c + 1)], X[c][0:E, :]).then_inc(c_gc, 1)

            C_STEPS = [c_x2, c_stats, c_norm, c_lo_part, c_shift, c_top2, c_gate_rows]

            def period(n, half, par, last=False, first=False):
                for item in ITEMS:
                    if item[0] == "e":
                        e = item[1]
                        if not isinstance(n, int) or issued(n + 1, e):
                            element(n + 1, half + par, 1 - par, e, idx(n + 1, e), bank_no(n + 1, e))
                    elif last and item[0] == "st" and item[2] == 1:
                        for i, f in enumerate(C_STEPS):
                            if C_AT["dve0"][i] == item[1]:
                                f(0, BANKS_C[0])

            for e in range(NE):
                if issued(0, e):
                    element(0, 0, 0, e, idx(0, e), bank_no(0, e))
            period(0, 0, 0, first=True)
            with dve.Fori(0, 3) as it:
                period(1 + 2 * it, it, 1)
                period(2 + 2 * it, it + 1, 0)
            period(NG - 1, 3, 1, last=True)

            def sum_up(ch):
                dve.wait_ge(d_tr, ch + 1)
                xs = x[:, bass.ds(TC * ch, TC), :].rearrange("p t d -> p (t d)")
                dve.tensor_tensor(xs, xs, obank[1][:, :], ALU.add).then_inc(d_acc, 1)

            def chunk(ch, first=False):
                for m in range(2 * E):
                    e = m // 2
                    dve.wait_ge(d_s, 2 * E * ch + m + 1)
                    if m % 2 == 0:
                        dve.wait_ge(ld_b[e % 4], 32 * ch + 16 * (e // 4 + 1))
                    dve.tensor_tensor(sw[m % 2][:, :], silu[m % 2][:, :], wbc[e % 4][:, :],
                                      ALU.mult).then_inc(d_sw, 1)
                    dve.wait_ge(d_u, 2 * E * ch + m + 1)
                    if not (first and m < 2):
                        dve.wait_ge(d_lo, 2 * E * ch + m - 1)
                    dve.wait_ge(d_sw, 2 * E * ch + m + 1)
                    dve.tensor_tensor(gg[m % 2][:, :], sw[m % 2][:, :], pair[m % 2][:, 0, :],
                                      ALU.mult).then_inc(d_g, 1)
                    if m == LAGD + 1 and not first:
                        sum_up(ch - 1)
                    if first and m == 1:
                        element(NG + 1, 4, 1, O1, idx(NG + 1, O1), bank_no(NG + 1, O1))
                    if first:
                        for i, f in enumerate(C_STEPS):
                            if C_AT["dve1"][i] == m:
                                f(1, BANKS_C[1])

            chunk(0, first=True)
            with dve.Fori(1, B * NC_) as ch:
                chunk(ch)
            sum_up(B * NC_ - 1)

        @block.tensor
        def _(pe):
            pe.wait_ge(cst, 12)

            def transposes(b, k):
                for c in range(NC_):
                    for i in range(TC):
                        last = pe.transpose(tr_bank(b, k, c)[:, P * i:P * (i + 1)],
                                            h_a[b][:, TC * c + i, :], ident[:, :])
                    last.then_inc(a_tr, 1)

            for b in range(B):
                pe.wait_ge(a_h, b + 1)
                for i in range(T):
                    last = pe.matmul(BK[4 * b][:, 0:HID], h_a[b][:, i, :], h_a[b][:, i, :],
                                     start=i == 0, stop=i == T - 1)
                last.then_inc(a_g, 1)
                transposes(b, 2 * b)
            pe.wait_ge(ld_w, 16 * 6)
            for b in range(B):
                pe.wait_ge(a_gs, b + 1)
                pe.matmul(BK[4 * b + 3][:, 0:HID], qmat[:, :], g_sb[b][:, :], start=True,
                          stop=True).then_inc(a_m, 1)
            for b in range(B):
                pe.wait_ge(a_ms, b + 1)
                pe.wait_ge(a_ht, 2 * (b + 1))
                for c in range(NC_):
                    for i in range(TC):
                        t = TC * c + i
                        last = pe.matmul(BK[4 * b + c][:, P * i:P * (i + 1)], ht_a[b][:, P * t:P * (t + 1)],
                                         m_sb[b][:, :], start=True, stop=True)
                    last.then_inc(a_att, 1)
            for b in range(B):
                pe.wait_ge(a_h, B + b + 1)
                transposes(b, 2 * B + 2 * b)
            for b in range(B):
                X = BK[4 * b:4 * b + 4]
                pe.wait_ge(a_ht, 2 * B + 2 * (b + 1))
                for bk, w0 in ((X[2], K0), (X[3], RK0)):
                    for c in range(NC_):
                        last = pe.matmul(bk[32 * c:32 * (c + 1), :], wqk_sb[:, w0:w0 + 32],
                                         ht_a[b][:, C2 * c:C2 * (c + 1)], start=True, stop=True)
                last.then_inc(a_qk, 1)
                for c in range(NC_):
                    if c:
                        pe.wait_ge(a_sum, 3 * b + 2)
                    for bk, w0 in ((X[0], QK0), (X[1], RQ0)):
                        last = pe.matmul(bk, wqk_sb[:, w0:w0 + P], ht_a[b][:, C2 * c:C2 * (c + 1)],
                                         start=True, stop=True)
                    last.then_inc(a_qk, 1)
                    if c == 0:
                        pe.wait_ge(a_sum, 3 * b + 1)
                        for i in range(T):
                            last = pe.matmul(X[2][:, 32 * i:32 * (i + 1)], ht_a[b][:, P * i:P * (i + 1)],
                                             wqk_sb[:, V0:V0 + 32], start=True, stop=True)
                        last.then_inc(a_v, 1)

            pe.wait_ge(a_lo, 3 * B)
            pe.wait_ge(a_vs, B)

            def element(n, half, par, e, no, bk):
                kind, u = STREAM[e]
                bk = S_BANKS[bk]
                if isinstance(n, int) and n >= NG:
                    pe.wait_ge(s_free, no)
                elif not (isinstance(no, int) and no < NSB):
                    pe.wait_ge(s_free, no - NSB + 1)
                if kind == "s":
                    i, k0, nb, heads = u
                    w = nb * P
                    if UNIT_OF[e] == 0:
                        pe.wait_ge(ld_s[par], 16 * 5 * (half + 1))
                    diag = k0 + nb - 1 == i
                    nh = len(heads)
                    o = bk[:, 0:w * nh].rearrange("p (h k) -> p h k", h=nh)
                    last = pe.matmul(o, sq_stk[par][:, P * i:P * (i + 1)],
                                     sk_stk[par][:, heads[0]:heads[0] + nh, P * k0:P * k0 + w],
                                     start=True, stop=not diag)
                    if diag:
                        last = pe.matmul(o[:, :, w - P:w], ident_bf[:, :],
                                         mask_bf[:, :].unsqueeze(1).broadcast_to([P, nh, P]),
                                         start=False, stop=True)
                    last.then_inc(s_ready, 1)
                elif kind == "t":
                    g, c = (n, 0) if e == T0 else (n - 1, 1)
                    pe.wait_ge(m_neg, 2 * g + c + 1)
                    pe.transpose(bk[0:32, 0:P], neg[:, c, :, :, :].rearrange("p h s i -> p (h s i)"),
                                 ident[:, :]).then_inc(s_ready, 1)
                else:
                    g, c = (n - 1, 0) if e == O0 else (n - 2, 1)
                    pe.wait_ge(o_cp, 2 * g + c + 1)
                    for i in range(TC):
                        last = pe.transpose(bk[:, P * i:P * (i + 1)], o_sb[c][:, P * i:P * (i + 1)],
                                            ident[:, :])
                    last.then_inc(s_ready, 1)

            def times_v(n, par, s):
                c, j = SLOTS[s]
                q0, w = slot_cols(c, j)
                if DIAG[s]:
                    pe.wait_ge(k_done, NMASK * n + MASK_NO[s] + 2)
                pe.wait_ge(e_done, NU * n + 2 * s + 2)
                for r in range(REP):
                    last = pe.matmul(o_acc[32 * r:32 * (r + 1), q0:C2], v_stk[par][:, j, :],
                                     pt[:, (2 * s + r // 2) % NPB, r % 2, 0:w],
                                     start=j == 0, stop=j == TC * (c + 1) - 1)
                last.then_inc(pv_done, 1)

            def c_attn(b, X):
                pe.wait_ge(s_free, TAIL if b == 0 else len(_ORDER))
                if b == 1:
                    pe.wait_ge(e_done, NU * NG)
                for c in range(NC_):
                    for i in range(TC):
                        src = otok[:, TC * c + i, NKV * b:NKV * (b + 1), :].rearrange("p g d -> p (g d)")
                        last = pe.transpose(X[c][:, P * i:P * (i + 1)], src, ident[:, :])
                    last.then_inc(c_tr, 1)

            def c_wo_mm(b, X):
                for c in range(NC_):
                    pe.wait_ge(c_cp, 4 * b + c + 1)
                    for i in range(TC):
                        t = TC * c + i
                        last = pe.matmul(X[c][:, P * i:P * (i + 1)], ot[b][:, P * t:P * (t + 1)],
                                         wo_sb[:, :], start=True, stop=True)
                    last.then_inc(c_wo, 1)

            def c_h2_tr(b, X):
                pe.wait_ge(c_h, b + 1)
                for c in range(NC_):
                    for i in range(TC):
                        last = pe.transpose(X[c][:, P * i:P * (i + 1)], h2[:, T * b + TC * c + i, :], ident[:, :])
                    last.then_inc(c_tr, 1)

            def c_logits(b, X):
                pe.wait_ge(c_cp, 4 * (b + 1))
                pe.wait_ge(c_hi, 2 * b + 1)
                for i in range(T):
                    last = pe.matmul(X[0][:, E * i:E * (i + 1)], h2t[:, S * b + P * i:S * b + P * (i + 1)],
                                     gate_sb[:, :], start=True, stop=True)
                last.then_inc(c_lg, 1)

            def c_gate_tr(b, X):
                pe.wait_ge(c_w, b + 1)
                pe.wait_ge(c_hi, 2 * (b + 1))
                for c in range(NC_):
                    for i in range(TC):
                        last = pe.transpose(X[c][0:E, P * i:P * (i + 1)], gate_w[:, T * b + TC * c + i, :],
                                            ident[:, :])
                    last.then_inc(c_gt, 1)

            C_STEPS = [c_attn, c_wo_mm, c_h2_tr, c_logits, c_gate_tr]

            def period(n, half, par, first=False, last=False):
                for item in ITEMS:
                    kind, s = item[0], item[1]
                    if kind == "e":
                        if not isinstance(n, int) or issued(n + 1, s):
                            element(n + 1, half + par, 1 - par, s, idx(n + 1, s), bank_no(n + 1, s))
                    elif kind == "st":
                        t = item[2]
                        c, j = SLOTS[s]
                        q0, w = slot_cols(c, j)
                        if s == 0 and t == 0:
                            pe.wait_ge(ld_t[par], 16 * 7 * (half + 1))
                        if j == 0 and t == 0:
                            pe.wait_ge(ld_m[c][par], 64 * (half + 1))
                        v = 2 * s + t
                        if not (first and v < 2):
                            pe.wait_ge(e_done, NU * n + v - 1)
                        for jj in range(2):
                            ins = pe.matmul(pair[v % 2][:, jj, 0:w], tk_stk[par][64 * jj:64 * jj + 34, P * j:P * (j + 1)],
                                            tq_stk[par][t][64 * jj:64 * jj + 34, C2 * c + q0:C2 * (c + 1)],
                                            start=True, stop=True)
                        ins.then_inc(t_done, 1)
                        if last and t == 1:
                            for i, f in enumerate(C_STEPS):
                                if C_AT["pe0"][i] == s:
                                    f(0, BANKS_C[0])
                    elif kind == "pv":
                        if s >= LAG:
                            if s - LAG == 0 and not first:
                                pe.wait_ge(o_cp, 2 * n)
                            if s - LAG == TC:
                                pe.wait_ge(o_cp, 2 * n + 1)
                            times_v(n, par, s - LAG)
                        elif not first:
                            times_v(n - 1, 1 - par, NS - LAG + s)

            for e in range(NE):
                if issued(0, e):
                    element(0, 0, 0, e, idx(0, e), bank_no(0, e))
            pe.wait_ge(cst, 16)
            period(0, 0, 0, first=True)
            with pe.Fori(0, 3) as it:
                period(1 + 2 * it, it, 1)
                period(2 + 2 * it, it + 1, 0)
            period(NG - 1, 3, 1, last=True)
            for s in range(NS - LAG, NS):
                times_v(NG - 1, 1, s)

            pe.wait_ge(w_lo, 3)
            pe.wait_ge(c_lo, 1)
            pe.wait_ge(o_cp, 2 * NG)
            pe.wait_ge(c_gc, 2)

            def down(ch, m):
                e, f = m // 2, m % 2
                pe.wait_ge(d_hi, 2 * E * ch + m + 1)
                for w in (w2h, w2l):
                    pe.matmul(obank[0][:, :], w[:, e, f, :], gh[m % 4][:, :], start=m == 0 and w is w2h,
                              stop=False)
                pe.wait_ge(d_lo, 2 * E * ch + m + 1)
                pe.matmul(obank[0][:, :], w2h[:, e, f, :], gl[m % 4][:, :], start=False,
                          stop=m == 2 * E - 1).then_inc(d_dn, 1)

            def sum_transposes(ch):
                pe.wait_ge(d_o, ch + 1)
                for i in range(TC):
                    last = pe.transpose(obank[1][:, P * i:P * (i + 1)], out_t[:, P * i:P * (i + 1)], ident[:, :])
                last.then_inc(d_tr, 1)

            def chunk(ch, first=False):
                for m in range(2 * E):
                    for which, bk, free, ready in ((0, bank[m % 2][:, :], d_s, d_a),
                                                   (1, pair[m % 2][:, 0, :], d_g, d_u)):
                        if not (first and m < 2):
                            pe.wait_ge(free, 2 * E * ch + m - 1)
                        col = which * FFN + m % 2 * P
                        for k, (w, h) in enumerate(((w13h, h2h), (w13h, h2l), (w13l, h2h))):
                            last = pe.matmul(bk, w[:, m // 2, col:col + P], h[:, bass.ds(C2 * ch, C2)],
                                             start=k == 0, stop=k == 2)
                        last.then_inc(ready, 1)
                    if m >= LAGD:
                        if m == LAGD and not first:
                            pe.wait_ge(d_o, ch)
                        down(ch, m - LAGD)
                    elif not first:
                        down(ch - 1, 2 * E - LAGD + m)
                    if m == LAGD and not first:
                        sum_transposes(ch - 1)
                    if first and m == 0:
                        element(NG + 1, 4, 1, O1, idx(NG + 1, O1), bank_no(NG + 1, O1))
                    if first:
                        for i, f in enumerate(C_STEPS):
                            if C_AT["pe1"][i] == m:
                                f(1, BANKS_C[1])

            chunk(0, first=True)
            pe.wait_ge(c_lo, B)
            with pe.Fori(1, B * NC_) as ch:
                chunk(ch)
            for m in range(2 * E - LAGD, 2 * E):
                down(B * NC_ - 1, m)
            sum_transposes(B * NC_ - 1)

    return nc


_INS = ["L0_attn_hidden_states", "L0_attn_queries", "L0_ffn_ln1_w", "L0_ffn_ln2_w", "L0_ffn_wqkv",
        "L0_ffn_wo", "L0_ffn_gate_w", "L0_ffn_w13", "L0_ffn_w2"]


def _rope_tables():
    import numpy as np
    inv = (np.float32(1.0) / np.float32(10000.0) ** (np.arange(0, HD, 2, dtype=np.float32) / np.float32(HD)))
    ang = np.arange(S, dtype=np.float32)[:, None] * inv.astype(np.float32)[None, :]
    ang = np.concatenate([ang, ang], axis=1).T
    cos, sin = np.cos(ang).astype(np.float32), np.sin(ang).astype(np.float32)
    sin = sin * np.where(np.arange(HD) < HD // 2, -1.0, 1.0).astype(np.float32)[:, None]
    scale = np.float32(HD ** -0.5)
    cq, sq = np.tile(cos * scale, (NH, 1)), np.tile(sin * scale, (NH, 1))

    def halves(a):
        a = np.tile(a, (NKV, 1))
        return np.concatenate([a[:, C2 * c:C2 * (c + 1)] for c in range(NC_)], axis=0)
    return [np.ascontiguousarray(a, dtype=np.float32) for a in (cq, sq, halves(cos), halves(sin))]


def kernel(**inputs):
    import numpy as np
    import concourse.bacc as bacc
    from concourse.bass_utils import run_bass_kernel_spmd

    a = {k: np.asarray(inputs[k]) for k in _INS}
    turned = (np.arange(HD) + HD // 2) % HD
    w = a["L0_ffn_wqkv"].T
    nq, nk = NH * HD, NKV * HD
    wq, wk, wv = w[:, :nq], w[:, nq:nq + nk], w[:, nq + nk:]
    wrq = wq.reshape(HID, NH, HD)[:, :, turned].reshape(HID, nq)
    wrk = wk.reshape(HID, NKV, HD)[:, :, turned].reshape(HID, nk)
    arrays = {
        "x_in": a["L0_attn_hidden_states"],
        "queries": a["L0_attn_queries"],
        "ln1": a["L0_ffn_ln1_w"].reshape(HID, 1),
        "ln2": a["L0_ffn_ln2_w"].reshape(HID, 1),
        "wqk": np.concatenate([wq, wrq, wk, wrk, wv], axis=1),
        "wo_t": a["L0_ffn_wo"].T,
        "gate_t": a["L0_ffn_gate_w"].T,
        "w13_t": a["L0_ffn_w13"].transpose(0, 2, 1),
        "w2_t": a["L0_ffn_w2"].transpose(0, 2, 1),
    }
    for name, table in zip(("cos_q", "sin_q", "cos_k", "sin_k"), _rope_tables()):
        arrays[name] = table
    arrays = {k: np.ascontiguousarray(v) for k, v in arrays.items()}
    nc = bacc.Bacc("TRN2", target_bir_lowering=False, num_devices=1)
    args = [nc.dram_tensor(k, v.shape, mybir.dt.from_np(v.dtype), kind="ExternalInput").ap()
            for k, v in arrays.items()]
    args.append(nc.dram_tensor("result", (B, S, HID), mybir.dt.float32, kind="ExternalOutput").ap())
    build_program(nc, *args)
    r = run_bass_kernel_spmd(nc, [arrays], core_ids=[0])
    return r.results[0]["result"]
```

```python
import concourse.bass as bass
from concourse import mybir
from contextlib import ExitStack

P = 128
B, S, HID = 2, 1024, 128
NH, NKV, HD = 16, 4, 8
REP = NH // NKV
E, FFN = 8, 256
EPS = 1e-5
T = S // P
C2 = 512
NC_ = S // C2
TC = C2 // P
NG = B * NKV
QK0, RQ0, K0, RK0, V0 = 0, 128, 256, 288, 320
WQK = 352
MASKED = -3.0e38

S_UNITS = []
for _i in range(T):
    for _k0, _nb in ((0, min(_i + 1, TC)), (TC, _i + 1 - TC)):
        if _nb > 0:
            _per = TC // _nb if _nb < 3 else 1
            for _h in range(0, REP, _per):
                S_UNITS.append((_i, _k0, _nb, list(range(_h, _h + _per))))
N_LOW = sum(1 for u in S_UNITS if u[0] < TC)
STREAM = [("s", u) for u in S_UNITS]
for _pos, _what in ((2, ("t", 1)), (14, ("o", 1)), (N_LOW + 6, ("t", 0)), (32, ("o", 0))):
    STREAM.insert(_pos, _what)
NSB = 3
NE = len(STREAM)
assert NE % NSB == 0
T1, T0, O1, O0 = (STREAM.index(x) for x in (("t", 1), ("t", 0), ("o", 1), ("o", 0)))
UNIT_OF = [sum(1 for x in STREAM[:e] if x[0] == "s") for e in range(NE)]


def issued(n, e):
    if STREAM[e][0] == "s":
        return n < NG
    if e == T0:
        return n < NG
    return n >= {T1: 1, O0: 1, O1: 2}[e] and (n < NG + (2 if e == O1 else 1))


_ORDER = [(n, e) for n in range(NG + 2) for e in range(NE) if issued(n, e)]
TAIL = _ORDER.index((NG, T1))


def idx(n, e):
    return _ORDER.index((n, e)) if isinstance(n, int) else n * NE - 4 + e


def bank_no(n, e):
    if isinstance(n, int):
        return NSB - 1 if n >= NG else idx(n, e) % NSB
    return (e - 4) % NSB


assert all(idx(n, e) == n * NE - 4 + e for n in (2, 5, NG - 1) for e in range(NE))
SLOTS = [(c, j) for c in range(NC_) for j in range(TC * (c + 1))]
NS = len(SLOTS)
NU = 2 * NS
NPB = 6
LAG = 2


def slot_cols(c, j):
    q0 = max(0, (j - TC * c) * P)
    return q0, C2 - q0


DIAG = [j >= TC * c for c, j in SLOTS]
MASK_NO = [2 * sum(DIAG[:s]) for s in range(NS)]
NMASK = 2 * sum(DIAG)




def period_items():
    main = []
    for s, (c, j) in enumerate(SLOTS):
        w = slot_cols(c, j)[1] / C2
        main += [(0.45 * w, ("st", s, 0)), (0.45 * w, ("st", s, 1)),
                 (0.92 * slot_cols(*SLOTS[(s - LAG) % NS])[1] / C2, ("pv", s))]
    cols = [x[1][2] * len(x[1][3]) * P / C2 if x[0] == "s" else 0.3 if x[0] == "t" else 1.2 for x in STREAM]
    on_pe = [0.22 * c + (0.15 if x[0] == "s" else 0) for c, x in zip(cols, STREAM)]
    on_dve = [0.54 * c + 0.13 for c in cols]
    total, read = sum(m[0] for m in main), sum(on_dve)
    items, e, pe_t, dve_t, done, main_done = [], 0, 0.0, 0.0, [], 0.0
    for k, (cost, item) in enumerate(main):
        while e < NE and (e < NSB or done[e - NSB] <= pe_t) \
                and sum(on_dve[:e]) / read <= (main_done + 0.5 * cost) / total + 0.02:
            items.append(("e", e))
            pe_t += on_pe[e]
            dve_t = max(dve_t, pe_t + 0.1) + on_dve[e]
            done.append(dve_t)
            e += 1
        items.append(item)
        pe_t += cost
        main_done += cost
    return items + [("e", k) for k in range(e, NE)]


ITEMS = period_items()
LAGD = 3


def build_program(nc, x_in, queries, ln1, ln2, wqk, wo_t, gate_t, w13_t, w2_t,
                  cos_q, sin_q, cos_k, sin_k, out):
    F, FR, BF = mybir.dt.float32, mybir.dt.float32r, mybir.dt.bfloat16
    ALU, ACT, AX = mybir.AluOpType, mybir.ActivationFunctionType, mybir.AxisListType

    ctx = ExitStack()
    with ctx:
        def sb(name, shape, dt=F, scope=ctx):
            return scope.enter_context(nc.sbuf_tensor(name, shape, dt))

        def sem(name):
            return ctx.enter_context(nc.semaphore(name))

        q_scr = nc.dram_tensor("q_scr", [NG * REP, 2, HD, S], F, kind="Internal").ap()
        k_scr = nc.dram_tensor("k_scr", [4, NG * HD, S], F, kind="Internal").ap()
        g_scr = nc.dram_tensor("g_scr", [E, B * S], F, kind="Internal").ap()

        x = sb("x", [P, B * T, HID])
        y = sb("y", [P, B * T, HID])
        otok = sb("otok", [P, T, NG, 32])
        w13h, w13l = sb("w13h", [P, E, 2 * FFN], FR), sb("w13l", [P, E, 2 * FFN], FR)
        w2h, w2l = sb("w2h", [P, E, 2, HID], FR), sb("w2l", [P, E, 2, HID], FR)
        qmat = sb("qmat", [P, HID])
        ln1c, ln2c = sb("ln1c", [P, 1]), sb("ln2c", [P, 1])
        wqk_sb = sb("wqk_sb", [P, WQK])
        wo_sb = sb("wo_sb", [P, HID])
        gate_sb = sb("gate_sb", [P, E])
        ident = sb("ident", [P, P])
        ident_bf, mask_bf = sb("ident_bf", [P, P], BF), sb("mask_bf", [P, P], BF)
        tick = sb("tick", [P, 2])
        tri = sb("tri", [P, E, E])
        v_all = sb("v_all", [P, NG, T, 32])
        warm = sb("warm", [P, 1])
        m_half = sb("m_half", [P, T])
        stats = sb("stats", [P, B * T, 6])
        mv = sb("mv", [P, B * T, 2])
        var_t = sb("var_t", [P, B, 2, T])
        rstd = sb("rstd", [P, B, 2, T])
        rms = sb("rms", [P, B * T])
        gate_w = sb("gate_w", [P, B * T, E])
        mx = sb("mx", [P, NC_, TC, REP])
        mx2 = sb("mx2", [P, TC, REP])
        neg = sb("neg", [P, NC_, REP, 2, TC])
        m_rows = [sb(f"m_rows{c}", [32, P]) for c in range(NC_)]
        o_sb = [sb(f"o_sb{c}", [P, C2]) for c in range(NC_)]
        o_rec = [sb(f"o_rec{c}", [P, TC, REP]) for c in range(NC_)]

        s_ab = ExitStack()
        w13r, w2r = sb("w13r", [P, E, 2 * FFN], F, s_ab), sb("w2r", [P, E, 2, HID], F, s_ab)
        sk_stk = [sb(f"sk_stk{i}", [P, REP, S], FR, s_ab) for i in range(2)]

        s_a = ExitStack()
        h_a, ht_a, g_sb, m_sb, q_hi, q_lo, k_hi, k_lo = [], [], [], [], [], [], [], []
        for b in range(B):
            h_a.append(sb(f"h_a{b}", [P, T, HID], F, s_a))
            ht_a.append(sb(f"ht_a{b}", [P, S], F, s_a))
            g_sb.append(sb(f"g_sb{b}", [P, HID], F, s_a))
            m_sb.append(sb(f"m_sb{b}", [P, HID], F, s_a))
            q_hi.append(sb(f"q_hi{b}", [P, S], FR, s_a))
            q_lo.append(sb(f"q_lo{b}", [P, S], FR, s_a))
            k_hi.append(sb(f"k_hi{b}", [64, C2], FR, s_a))
            k_lo.append(sb(f"k_lo{b}", [64, C2], FR, s_a))
            if b == 0:
                cq, sq = sb("cq", [P, S], F, s_a), sb("sq", [P, S], F, s_a)
                ck, sk = sb("ck", [64, C2], F, s_a), sb("sk", [64, C2], F, s_a)
                t_cos = [sb(f"t_cos{i}", [P, C2], F, s_a) for i in range(2)]
                t_sin = sb("t_sin", [P, C2], F, s_a)
        s_a.close()
        s_b = ExitStack()
        sq_stk = [sb(f"sq_stk{i}", [P, S], FR, s_b) for i in range(2)]
        tq_stk, tk_stk, v_stk = [], [], []
        for i in range(2):
            tq_stk.append([sb(f"tq_stk{i}{t}", [P, S], FR, s_b) for t in range(2)])
            tk_stk.append(sb(f"tk_stk{i}", [P, S], FR, s_b))
            v_stk.append(sb(f"v_stk{i}", [P, T, 32], F, s_b))
        pt = sb("pt", [P, NPB, 2, C2], F, s_b)
        s_b.close()
        s_ab.close()
        s_c = ExitStack()
        h2h, h2l = sb("h2h", [P, B * S], FR, s_c), sb("h2l", [P, B * S], FR, s_c)
        ot = [sb(f"ot{b}", [P, S], F, s_c) for b in range(B)]
        h2 = sb("h2", [P, B * T, HID], F, s_c)
        h2t = sb("h2t", [P, B * S], F, s_c)
        stats2, mv2 = sb("stats2", [P, T, 6], F, s_c), sb("mv2", [P, T, 2], F, s_c)
        lg, ex = sb("lg", [P, T, E], F, s_c), sb("ex", [P, T, E], F, s_c)
        cmp1, cmp2 = sb("cmp1", [P, T, E, E], F, s_c), sb("cmp2", [P, T, E, E], F, s_c)
        r8 = sb("r8", [P, 2, T], F, s_c)
        gate_wt = [sb(f"gate_wt{b}", [E, S], F, s_c) for b in range(B)]
        wbc = [sb(f"wbc{i}", [P, C2], F, s_c) for i in range(4)]
        silu = [sb(f"silu{i}", [P, C2], F, s_c) for i in range(2)]
        sw = [sb(f"sw{i}", [P, C2], F, s_c) for i in range(2)]
        gg = [sb(f"gg{i}", [P, C2], F, s_c) for i in range(2)]
        gh = [sb(f"gh{i}", [P, C2], FR, s_c) for i in range(4)]
        gl = [sb(f"gl{i}", [P, C2], FR, s_c) for i in range(4)]
        out_t = sb("out_t", [P, C2], F, s_c)
        s_c.close()

        bank = [ctx.enter_context(nc.psum_tensor(f"bank{i}", [P, C2], F)) for i in range(2)]
        pair = [ctx.enter_context(nc.psum_tensor(f"pair{i}", [P, 2, C2], F)) for i in range(2)]
        obank = [ctx.enter_context(nc.psum_tensor(f"obank{i}", [P, C2], F)) for i in range(2)]
        BK = [bank[0][:, :], bank[1][:, :], pair[0][:, 0, :], pair[0][:, 1, :],
              pair[1][:, 0, :], pair[1][:, 1, :], obank[0][:, :], obank[1][:, :]]

        ld_x = [sem(f"ld_x{b}") for b in range(B)]
        ld_w = sem("ld_w")
        ld_rope = sem("ld_rope")
        ld_moe = sem("ld_moe")
        cst = sem("cst")
        zeroed = sem("zeroed")
        vq = sem("vq")
        a_var = sem("a_var")
        a_std = sem("a_std")
        a_h = sem("a_h")
        a_tr = sem("a_tr")
        a_ht = sem("a_ht")
        a_g, a_gs = sem("a_g"), sem("a_gs")
        a_m, a_ms = sem("a_m"), sem("a_ms")
        a_att, a_x1 = sem("a_att"), sem("a_x1")
        a_qk = [sem(f"a_qk{b}") for b in range(B)]
        a_v, a_vs = sem("a_v"), sem("a_vs")
        a_mul = sem("a_mul")
        a_sum = sem("a_sum")
        a_hi = sem("a_hi")
        a_lo = sem("a_lo")
        scr_q = [sem(f"scr_q{b}") for b in range(B)]
        scr_k = [sem(f"scr_k{b}") for b in range(B)]
        w_hi, w_lo = sem("w_hi"), sem("w_lo")
        ld_s = [sem(f"ld_s{i}") for i in range(2)]
        ld_t = [sem(f"ld_t{i}") for i in range(2)]
        s_ready, s_free = sem("s_ready"), sem("s_free")
        m_neg = sem("m_neg")
        n_hi, n_mx = sem("n_hi"), sem("n_mx")
        n_rc = sem("n_rc")
        ld_m = [[sem(f"ld_m{c}{i}") for i in range(2)] for c in range(NC_)]
        t_done = sem("t_done")
        e_done = sem("e_done")
        k_done = sem("k_done")
        pv_done = sem("pv_done")
        o_cp = sem("o_cp")
        c_tr, c_cp = sem("c_tr"), sem("c_cp")
        c_wo, c_h = sem("c_wo"), sem("c_h")
        c_var, c_rms = sem("c_var"), sem("c_rms")
        c_lg = sem("c_lg")
        c_sh, c_ex = sem("c_sh"), sem("c_ex")
        c_hi, c_lo, c_w = sem("c_hi"), sem("c_lo"), sem("c_w")
        c_gt, c_gc = sem("c_gt"), sem("c_gc")
        cv = sem("cv")
        gw_st = sem("gw_st")
        ld_b = [sem(f"ld_b{i}") for i in range(4)]
        d_a, d_u = sem("d_a"), sem("d_u")
        d_s, d_sw, d_g = sem("d_s"), sem("d_sw"), sem("d_g")
        d_hi, d_lo = sem("d_hi"), sem("d_lo")
        d_dn = sem("d_dn")
        d_o, d_tr = sem("d_o"), sem("d_tr")
        d_x = sem("d_x")
        d_acc = sem("d_acc")
        st = sem("st")
        block = ctx.enter_context(nc.Block())

        out_v = out.rearrange("b (t p) d -> (b t) p d", p=P)
        x_v = x_in.rearrange("b (t p) d -> b p t d", p=P)

        K_DONE = Q_DONE = 16 * 2 * NC_
        S_BANKS = [BK[0], BK[1], BK[7]]
        o_acc = obank[0]

        XA = [(BK[0], BK[1], BK[6], BK[7]), (BK[2], BK[3], BK[4], BK[5])]

        BANKS_C = [(BK[0], BK[1]), (BK[3], BK[5])]
        C_AT = {"act": ((2, 13, 17), (4, 15, 19)),
                "dve": ((2, 2, 3, 3, 3, 4, 4, 6, 6, 7, 8, 8, 8, 8, 8, 8, 10, 10),
                        (6, 7, 8, 9, 10, 12, 13, 16, 17, 18, 20, 21, 22, 23, 24, 25, 28, 29)),
                "root": (3, 10), "pe": ((0, 2, 6, 7, 10), (3, 5, 14, 17, 27))}

        def stage_c(engine, steps, b, at):
            for i, f in enumerate(steps):
                if C_AT[engine][b][i] == at:
                    f(b, BANKS_C[b])

        @block.sync
        def _(sp):
            sp.dma_start(x[:, 0:T, :], x_v[0]).then_inc(ld_x[0], 16)
            for dst, src in ((qmat[:, :], queries), (ln1c[:, :], ln1), (ln2c[:, :], ln2),
                             (wqk_sb[:, :], wqk), (wo_sb[:, :], wo_t), (gate_sb[:, :], gate_t)):
                sp.dma_start(dst, src).then_inc(ld_w, 16)
            sp.dma_start(x[:, T:2 * T, :], x_v[1]).then_inc(ld_x[1], 16)
            for dst, src in ((cq, cos_q), (sq, sin_q), (ck, cos_k), (sk, sin_k)):
                sp.dma_start(dst[:, :], src).then_inc(ld_rope, 16)
            sp.dma_start(w13r[:, :, :], w13_t.rearrange("e h f -> h e f")).then_inc(ld_moe, 16)
            sp.dma_start(w2r[:, :, :, :],
                         w2_t.rearrange("e (t p) h -> p e t h", p=P)).then_inc(ld_moe, 16)
            def write_k(b):
                sp.wait_ge(a_hi, 3 * b + 1)
                sp.wait_ge(a_lo, 3 * b + 1)
                rows_ = NKV * HD
                kv = k_scr.rearrange("(s r) m n -> m s r n", r=2)[rows_ * b:rows_ * (b + 1)]
                for s, part in enumerate((k_hi[b], k_lo[b])):
                    for c in range(NC_):
                        sp.dma_start(kv[:, s, :, C2 * c:C2 * (c + 1)],
                                     part[32 * c:32 * (c + 1), :].bitcast(F).unsqueeze(1)
                                     .broadcast_to([32, 2, C2])).then_inc(scr_k[b], 16)

            def write_q(b, c):
                sp.wait_ge(a_hi, 3 * b + 2 + c)
                sp.wait_ge(a_lo, 3 * b + 2 + c)
                for s, part in enumerate((q_hi[b], q_lo[b])):
                    sp.dma_start(q_scr[NKV * REP * b:NKV * REP * (b + 1), s, :, C2 * c:C2 * (c + 1)],
                                 part[:, C2 * c:C2 * (c + 1)].bitcast(F)).then_inc(scr_q[b], 16)

            def q_rows(n, r):
                return q_scr[bass.ds(REP * n + r, 1), :, :, :].rearrange("h s d n -> h (s d n)") \
                    .broadcast_to([2, 2 * HD * S])

            def k_rows(n):
                return k_scr[:, bass.ds(HD * n, HD), :]

            def load_sk(n, par):
                for r in range(REP):
                    sp.dma_start(sk_stk[par][32 * r:32 * (r + 1), r, :].bitcast(F), k_rows(n)).then_inc(ld_s[par], 16)

            def load_sq(n, par):
                for r in range(REP):
                    sp.dma_start(sq_stk[par][32 * r:32 * (r + 1), :].bitcast(F), q_rows(n, r)).then_inc(ld_s[par], 16)

            def load_t(n, par):
                for t in range(2):
                    for j in range(2):
                        r = 2 * t + j
                        sp.dma_start(tq_stk[par][t][64 * j:64 * j + 32, :].bitcast(F),
                                     q_rows(n, r)).then_inc(ld_t[par], 16)
                for j in range(2):
                    sp.dma_start(tk_stk[par][64 * j:64 * j + 32, :].bitcast(F),
                                 k_rows(n)).then_inc(ld_t[par], 16)
                sp.dma_start(v_stk[par][:, :, :].rearrange("p t n -> p (t n)"),
                             v_all[:, bass.ds(n, 1), :, :].rearrange("p g t n -> p (g t n)")).then_inc(ld_t[par], 16)

            def load_m(n, c, par):
                sp.wait_ge(s_free, idx(n, T0) + 1 if c == 0 else idx(n + 1, T1) + 1)
                for r in range(REP):
                    j = r % 2
                    sp.dma_start(
                        tq_stk[par][r // 2][64 * j + 32:64 * j + 34, C2 * c:C2 * (c + 1)].bitcast(F)
                        .rearrange("p (i n) -> p i n", i=TC),
                        m_rows[c][8 * r:8 * (r + 1), :]).then_inc(ld_m[c][par], 16)

            def next_t(n, par):
                if isinstance(n, int) and n == 0:
                    for sem_, count in ((scr_k[1], K_DONE), (scr_q[1], Q_DONE), (a_vs, B)):
                        sp.wait_ge(sem_, count)
                else:
                    sp.wait_ge(pv_done, NS * n)
                load_t(n + 1, 1 - par)

            def period(n, par, s_next=True, t_next=True, m_next=True):
                load_m(n, 1, par)
                if isinstance(n, int) and n == 0:
                    next_t(n, par)
                if s_next:
                    sp.wait_ge(s_ready, idx(n, NE - 1) + 1)
                    load_sk(n + 2, par)
                    load_sq(n + 2, par)
                if t_next and not (isinstance(n, int) and n == 0):
                    next_t(n, par)
                if m_next:
                    load_m(n + 1, 0, 1 - par)

            write_k(0)
            write_q(0, 0)
            write_q(0, 1)
            sp.wait_ge(zeroed, 1)
            sp.wait_ge(scr_k[0], K_DONE)
            load_sk(0, 0)
            sp.wait_ge(scr_q[0], Q_DONE)
            sp.wait_ge(a_vs, 1)
            load_sq(0, 0)
            write_k(1)
            write_q(1, 0)
            load_t(0, 0)
            sp.wait_ge(zeroed, 2)
            load_sk(1, 1)
            load_sq(1, 1)
            write_q(1, 1)
            load_m(0, 0, 0)
            period(0, 0)
            with sp.Fori(0, 2) as it:
                period(1 + 2 * it, 1)
                period(2 + 2 * it, 0)
            period(5, 1)
            period(6, 0, s_next=False)
            period(7, 1, s_next=False, t_next=False, m_next=False)

            def gate_store(b):
                sp.wait_ge(c_gc, 2 * (b + 1))
                sp.dma_start(g_scr[:, S * b:S * (b + 1)], gate_wt[b][:, :]).then_inc(gw_st, 16)
                sp.wait_ge(gw_st, 16 * (b + 1))

            def chunk(ch, first=False):
                for e in range(E):
                    if not (first and e < 4):
                        sp.wait_ge(d_sw, 2 * E * ch + 2 * (e - 4) + 2)
                    sp.dma_start(wbc[e % 4][:, :], g_scr[e:e + 1, bass.ds(C2 * ch, C2)]
                                 .broadcast_to([P, C2])).then_inc(ld_b[e % 4], 16)
                    if e == 5 and not first:
                        result(ch - 1)

            def result(ch):
                sp.wait_ge(d_acc, ch + 1)
                sp.dma_start(out_v[bass.ds(TC * ch, TC), :, :].rearrange("t p d -> p t d"),
                             x[:, bass.ds(TC * ch, TC), :]).then_inc(st, 16)

            gate_store(0)
            sp.wait_ge(pv_done, NS * NG)
            chunk(0, first=True)
            chunk(1)
            gate_store(1)
            with sp.Fori(2, B * NC_) as ch:
                chunk(ch)
            result(B * NC_ - 1)
            sp.wait_ge(st, 16 * B * NC_)

        @block.gpsimd
        def _(pool):
            pool.memset(warm[:, :], 1.0).then_inc(cst, 1)
            pool.memset(ident[:, :], 0.0).then_inc(cst, 1)
            pool.memset(ident_bf[:, :], 0.0).then_inc(cst, 1)
            pool.memset(mask_bf[:, :], 0.0).then_inc(cst, 1)
            pool.memset(tri[:, :, :], 1.0).then_inc(cst, 1)
            pool.memset(tick[:, :], 0.0).then_inc(cst, 1)
            pool.memset(m_half[:, :], -0.5).then_inc(cst, 1)
            pool.wait_ge(cst, 7)
            for m in (ident, ident_bf):
                pool.affine_select(out=m[:, :], in_=m[:, :], compare_op=ALU.not_equal, fill=1.0,
                                   base=0, pattern=[[-1, P]], channel_multiplier=1).then_inc(cst, 1)
            pool.affine_select(out=mask_bf[:, :], in_=mask_bf[:, :], compare_op=ALU.is_ge, fill=MASKED,
                               base=0, pattern=[[-1, P]], channel_multiplier=1).then_inc(cst, 1)
            pool.affine_select(out=tri[:, :, :], in_=tri[:, :, :], compare_op=ALU.is_gt, fill=0.0,
                               base=0, pattern=[[1, E], [-1, E]], channel_multiplier=0).then_inc(cst, 1)
            pool.memset(v_all[:, :, :, HD:HD + 1], 1.0).then_inc(cst, 1)
            pool.memset(v_all[:, :, :, HD + 1:32], 0.0).then_inc(cst, 1)
            for i in range(2):
                pool.memset(sk_stk[i][:, :, :].bitcast(F), 0.0).then_inc(zeroed, 1)
            pool.wait_ge(zeroed, 2)
            for n in range(3 * B):
                b, i = n // 3, n % 3
                t = t_cos[n % 2]
                cs = slice(C2 * (i - 1), C2 * i)
                if n:
                    pool.wait_ge(a_lo, n)
                pool.wait_ge(a_hi, n + 1)
                if i == 0:
                    pool.tensor_tensor(k_lo[b][:, :], t[0:64, :], k_hi[b][:, :].bitcast(F),
                                       ALU.subtract).then_inc(a_lo, 1)
                else:
                    pool.tensor_tensor(q_lo[b][:, cs], t[:, :], q_hi[b][:, cs].bitcast(F),
                                       ALU.subtract).then_inc(a_lo, 1)
            pool.wait_ge(a_lo, 3 * B)
            for i in range(2):
                for sem_, count in ((scr_k[i], K_DONE), (scr_q[i], Q_DONE), (a_vs, i + 1)):
                    pool.wait_ge(sem_, count)
                for j in range(2):
                    pool.wait_ge(cst, 13 + 2 * i + j)
                    pool.memset(tk_stk[i][64 * j + 32:64 * j + 34, :].bitcast(F), 1.0).then_inc(cst, 1)
            pool.wait_ge(cst, 17)
            pool.wait_ge(w_hi, 1)
            pool.tensor_tensor(w2l[:, :, :, :], w2r[:, :, :, :], w2h[:, :, :, :].bitcast(F),
                               ALU.subtract).then_inc(w_lo, 1)
            for i in range(2):
                pool.wait_ge(w_hi, 2 + i)
                e0, e1 = i * E // 2, (i + 1) * E // 2
                pool.tensor_tensor(w13l[:, e0:e1, :], w13r[:, e0:e1, :],
                                   w13h[:, e0:e1, :].bitcast(F), ALU.subtract).then_inc(w_lo, 1)

            def period(n, last=False):
                for s, (c, j) in enumerate(SLOTS):
                    if not DIAG[s]:
                        continue
                    for t in range(2):
                        v = 2 * s + t
                        if not (isinstance(n, int) and n + MASK_NO[s] + t == 0):
                            pool.wait_ge(k_done, NMASK * n + MASK_NO[s] + t)
                        pool.wait_ge(e_done, NU * n + v + 1)
                        blk = pt[:, v % NPB, :, 0:P]
                        pool.tensor_tensor(tick[:, 1:2], tick[:, 0:1], tick[:, 0:1], ALU.mult)
                        pool.affine_select(out=blk, in_=blk, compare_op=ALU.is_ge, fill=0.0, base=0,
                                           pattern=[[0, 2], [1, P]], channel_multiplier=-1).then_inc(k_done, 1)
                        if last and v == 2 * C_AT["root"][0] + 1:
                            c_root(0)

            def c_root(b):
                pool.wait_ge(c_var, b + 1)
                r = rms[:, T * b:T * (b + 1)]
                pool.tensor_tensor(r, r, m_half[:, :], ALU.pow).then_inc(c_rms, 1)

            period(0)
            with pool.Fori(1, NG - 1) as n:
                period(n)
            period(NG - 1, last=True)

            def chunk(ch, first=False):
                for m in range(2 * E):
                    pool.wait_ge(d_hi, 2 * E * ch + m + 1)
                    if not (first and m < 4):
                        pool.wait_ge(d_dn, 2 * E * ch + m - 3)
                    pool.tensor_tensor(gl[m % 4][:, :], gg[m % 2][:, :], gh[m % 4][:, :].bitcast(F),
                                       ALU.subtract).then_inc(d_lo, 1)
                    if first and m == C_AT["root"][1]:
                        c_root(1)

            chunk(0, first=True)
            with pool.Fori(1, B * NC_) as ch:
                chunk(ch)

        @block.scalar
        def _(act):
            def copy_t(b, n, banks, scale=None):
                for c in range(NC_):
                    act.wait_ge(a_tr, 2 * n + c + 1)
                    dst = ht_a[b][:, C2 * c:C2 * (c + 1)]
                    if scale is None:
                        act.copy(dst, banks[c]).then_inc(a_ht, 1)
                    else:
                        act.activation(dst, banks[c], ACT.Copy, scale=scale).then_inc(a_ht, 1)

            act.wait_ge(cst, 1)
            act.activation(warm[:, :], warm[:, :], ACT.Sqrt)

            def root(b, n):
                act.wait_ge(a_var, n)
                act.activation(var_t[:, b, :, :], var_t[:, b, :, :], ACT.Sqrt).then_inc(a_std, 1)

            root(0, 1)
            for b in range(B):
                X = XA[b]
                if b == 1:
                    root(0, 3)
                act.wait_ge(a_g, b + 1)
                act.copy(g_sb[b][:, :], X[0][:, 0:HID]).then_inc(a_gs, 1)
                if b == 0:
                    root(1, 2)
                copy_t(b, b, X[1:3])
                act.wait_ge(a_m, b + 1)
                act.copy(m_sb[b][:, :], X[3][:, 0:HID]).then_inc(a_ms, 1)
            copy_t(0, B, XA[0][2:4], ln1c[:, 0:1])
            root(1, 4)
            copy_t(1, B + 1, XA[1][2:4], ln1c[:, 0:1])

            for b in range(B):
                act.wait_ge(a_sum, 3 * b + 1)
                act.copy(k_hi[b][:, :], t_cos[(3 * b) % 2][0:64, :]).then_inc(a_hi, 1)
                act.wait_ge(a_sum, 3 * b + 2)
                act.copy(q_hi[b][:, 0:C2], t_cos[(3 * b + 1) % 2][:, :]).then_inc(a_hi, 1)
                act.wait_ge(a_sum, 3 * b + 3)
                act.copy(q_hi[b][:, C2:S], t_cos[(3 * b + 2) % 2][:, :]).then_inc(a_hi, 1)
                act.wait_ge(a_v, b + 1)
                act.wait_ge(cst, 13)
                act.copy(v_all[:, NKV * b:NKV * (b + 1), :, 0:HD].rearrange("p g t d -> p t g d"),
                         XA[b][0][:, 0:T * NKV * HD].rearrange("p (t g d) -> p t g d", t=T, g=NKV)
                         ).then_inc(a_vs, 1)
            act.wait_ge(ld_moe, 32)
            act.copy(w2h[:, :, :, :], w2r[:, :, :, :]).then_inc(w_hi, 1)
            for i in range(2):
                e0, e1 = i * E // 2, (i + 1) * E // 2
                act.copy(w13h[:, e0:e1, :], w13r[:, e0:e1, :]).then_inc(w_hi, 1)

            for sem_, count in ((scr_k[1], K_DONE), (scr_q[1], Q_DONE)):
                act.wait_ge(sem_, count)

            def o_copy(n, c):
                act.wait_ge(pv_done, NS * n + (TC if c == 0 else NS))
                if not (isinstance(n, int) and n == 0):
                    act.wait_ge(s_ready, idx(n, O0) + 1 if c == 0 else idx(n + 1, O1) + 1)
                act.copy(o_sb[c][:, :], o_acc[:, :]).then_inc(o_cp, 1)

            def c_ot(b, X):
                for c in range(NC_):
                    act.wait_ge(c_tr, 4 * b + c + 1)
                    act.copy(ot[b][:, C2 * c:C2 * (c + 1)], X[c]).then_inc(c_cp, 1)

            def c_h2t(b, X):
                for c in range(NC_):
                    cs = slice(S * b + C2 * c, S * b + C2 * (c + 1))
                    act.wait_ge(c_tr, 4 * b + 2 + c + 1)
                    act.activation(h2t[:, cs], X[c], ACT.Copy, scale=ln2c[:, 0:1]).then_inc(c_cp, 1)
                    act.activation(h2h[:, cs], X[c], ACT.Copy, scale=ln2c[:, 0:1]).then_inc(c_hi, 1)

            def c_exp(b, X):
                act.wait_ge(c_sh, b + 1)
                act.activation(ex[:, :, :], lg[:, :, :], ACT.Exp).then_inc(c_ex, 1)

            C_STEPS = [c_ot, c_h2t, c_exp]

            def period(n, first=False, last=False):
                for v in range(NU):
                    c, j = SLOTS[v // 2]
                    w = slot_cols(c, j)[1]
                    act.wait_ge(t_done, NU * n + v + 1)
                    if not (first and v < NPB):
                        act.wait_ge(pv_done, NS * n + (v - NPB) // 2 + 1)
                    act.activation(pt[:, v % NPB, :, 0:w], pair[v % 2][:, :, 0:w], ACT.Exp).then_inc(e_done, 1)
                    if v == 2 * LAG - 1 and not first:
                        o_copy(n - 1, 1)
                    if v == 2 * (TC + LAG) - 1:
                        o_copy(n, 0)
                    if last:
                        stage_c("act", C_STEPS, 0, v)

            period(0, first=True)
            with act.Fori(1, NG - 1) as n:
                period(n)
            period(NG - 1, last=True)
            o_copy(NG - 1, 1)

            def finish():
                act.copy(out_t[:, :], obank[0][:, :]).then_inc(d_o, 1)

            def hi_part(ch, m, first):
                act.wait_ge(d_g, 2 * E * ch + m + 1)
                if not (first and m < 4):
                    act.wait_ge(d_dn, 2 * E * ch + m - 3)
                act.copy(gh[m % 4][:, :], gg[m % 2][:, :]).then_inc(d_hi, 1)

            def chunk(ch, first=False):
                for m in range(2 * E):
                    if m == LAGD and not first:
                        act.wait_ge(d_dn, 2 * E * ch)
                        finish()
                    act.wait_ge(d_a, 2 * E * ch + m + 1)
                    if not (first and m < 2):
                        act.wait_ge(d_sw, 2 * E * ch + m - 1)
                    act.activation(silu[m % 2][:, :], bank[m % 2][:, :], ACT.Silu).then_inc(d_s, 1)
                    if m:
                        hi_part(ch, m - 1, first)
                    if isinstance(ch, int):
                        stage_c("act", C_STEPS, 1, 2 * E * ch + m)
                hi_part(ch, 2 * E - 1, False)

            chunk(0, first=True)
            chunk(1)
            with act.Fori(2, B * NC_) as ch:
                chunk(ch)
            act.wait_ge(d_dn, 2 * E * B * NC_)
            finish()

        @block.vector
        def _(dve):
            steps = [0]

            def link(ins):
                steps[0] += 1
                ins.then_inc(vq, 1)
                dve.wait_ge(vq, steps[0])

            def variance(b):
                for i in range(T * b, T * (b + 1)):
                    last = dve.bn_stats(stats[:, i, :], x[:, i, :])
                link(last)
                for i in range(T * b, T * (b + 1)):
                    last = dve.bn_aggr(mv[:, i, :], stats[:, i, :])
                link(last)

                dve.tensor_scalar(var_t[:, b, 0, :], mv[:, bt[b], 1], EPS, None, ALU.add)
                dve.tensor_scalar(var_t[:, b, 1, :], mv[:, bt[b], 1], 1.0 + EPS, EPS * EPS,
                                  ALU.mult, ALU.add).then_inc(a_var, 1)

            def inverse(b, n):
                dve.wait_ge(a_std, n)
                link(dve.reciprocal(rstd[:, b, :, :], var_t[:, b, :, :]))

            def normalise(b, dst, which, ready=None):
                for i in range(T):
                    k = T * b + i
                    last = dve.tensor_scalar(dst(i), x[:, k, :], mv[:, k, 0:1],
                                             rstd[:, b, which, i:i + 1], ALU.subtract, ALU.mult)
                    if ready is not None and i % TC == TC - 1:
                        last.then_inc(ready, 1)

            bt = [slice(T * b, T * (b + 1)) for b in range(B)]
            for b in range(B):
                dve.wait_ge(ld_x[b], 16)
                variance(b)
                inverse(b, b + 1)
                normalise(b, lambda i: h_a[b][:, i, :], 0, a_h)
            for b in range(B):
                for c in range(NC_):
                    dve.wait_ge(a_att, 2 * b + c + 1)
                    xs = x[:, T * b + TC * c:T * b + TC * (c + 1), :].rearrange("p t d -> p (t d)")
                    last = dve.tensor_tensor(xs, xs, XA[b][c], ALU.add)
                    last.then_inc(a_x1, 1)
                dve.wait_ge(a_x1, 2 * (b + 1))
                variance(b)
                inverse(b, B + b + 1)
                normalise(b, lambda i: h_a[b][:, i, :], 1, a_h)
            dve.wait_ge(ld_rope, 64)

            for n in range(3 * B):
                b, i = n // 3, n % 3
                X = XA[b]
                if i == 0:
                    rows_, direct, turned, cos, sin = 64, X[2][0:64, :], X[3][0:64, :], ck[:, :], sk[:, :]
                else:
                    cs = slice(C2 * (i - 1), C2 * i)
                    rows_, direct, turned, cos, sin = P, X[2 * i - 2], X[2 * i - 1], cq[:, cs], sq[:, cs]
                tc_, ts_ = t_cos[n % 2][0:rows_, :], t_sin[0:rows_, :]
                if n >= 2:
                    dve.wait_ge(a_lo, n - 1)
                dve.wait_ge(a_qk[b], i + 1)
                dve.tensor_tensor(tc_, direct, cos, ALU.mult)
                if n:
                    dve.wait_ge(a_sum, n)
                dve.tensor_tensor(ts_, turned, sin, ALU.mult).then_inc(a_mul, 1)
                dve.wait_ge(a_mul, n + 1)
                dve.tensor_tensor(tc_, tc_, ts_, ALU.add).then_inc(a_sum, 1)
            for b in range(B):
                normalise(b, lambda i: y[:, T * b + i, :], 0)
            def negate(n, c):
                src = mx[:, c, :, :].rearrange("p i h -> p h i")
                dve.tensor_scalar(neg[:, c, :, 0, :].bitcast(FR), src, -1.0, None, ALU.mult).then_inc(n_hi, 1)
                dve.wait_ge(n_hi, 2 * n + c + 1)
                dve.scalar_tensor_tensor(neg[:, c, :, 1, :].bitcast(FR), src, -1.0, neg[:, c, :, 0, :],
                                         ALU.mult, ALU.subtract).then_inc(m_neg, 1)

            def element(n, half, par, e, no, bk):
                kind, u = STREAM[e]
                dve.wait_ge(s_ready, no + 1)
                src = S_BANKS[bk]
                if kind == "s":
                    i, k0, nb, heads = u
                    w = nb * P
                    dst = mx[:, i // TC, i % TC, heads[0]:heads[-1] + 1] if k0 == 0 \
                        else mx2[:, i - TC, heads[0]:heads[-1] + 1]
                    dve.reduce_max(dst, src[:, 0:w * len(heads)].rearrange("p (h k) -> p h k", h=len(heads)),
                                   AX.X).then_inc(s_free, 1)
                    if UNIT_OF[e] == N_LOW - 1:
                        dve.wait_ge(s_free, no + 1)
                        negate(n, 0)
                    if e == NE - 1:
                        dve.wait_ge(s_free, no + 1)
                        dve.tensor_tensor(mx[:, 1, :, :], mx[:, 1, :, :], mx2[:, :, :], ALU.max).then_inc(n_mx, 1)
                        dve.wait_ge(n_mx, n + 1)
                        negate(n, 1)
                elif e == T0:
                    rows(n, half, par, 0, src)
                elif e == T1:
                    rows(n - 1, half - (1 - par), 1 - par, 1, src)
                else:
                    o_norm(n - 1 if e == O0 else n - 2, 0 if e == O0 else 1, src)

            def rows(n, half, par, c, src):
                if not (isinstance(n, int) and n == 0):
                    dve.wait_ge(ld_m[c][1 - par], 64 * (half + par))
                dve.tensor_copy(m_rows[c][:, :], src[0:32, 0:P]).then_inc(s_free, 1)

            def o_norm(n, c, bk):
                src = bk.rearrange("p (i h d) -> p i h d", i=TC, h=REP)
                dve.reciprocal(o_rec[c][:, :, :], src[:, :, :, HD]).then_inc(n_rc, 1)
                dve.wait_ge(n_rc, 2 * n + c + 1)
                dst = otok[:, TC * c:TC * (c + 1), bass.ds(n, 1), :].rearrange("p i g (h d) -> p (i g) h d", h=REP)
                dve.tensor_tensor(dst, src[:, :, :, 0:HD],
                                  o_rec[c][:, :, :].unsqueeze(3).broadcast_to([P, TC, REP, HD]),
                                  ALU.mult).then_inc(s_free, 1)

            c_steps = [0]

            def c_link(ins):
                c_steps[0] += 1
                ins.then_inc(cv, 1)
                dve.wait_ge(cv, c_steps[0])

            def c_x2(c):
                def step(b, X):
                    dve.wait_ge(c_wo, 2 * b + c + 1)
                    ys = y[:, T * b + TC * c:T * b + TC * (c + 1), :].rearrange("p t d -> p (t d)")
                    c_link(dve.tensor_tensor(ys, ys, X[c], ALU.add))
                return step

            def c_stats(c):
                def step(b, X):
                    for i in range(TC * c, TC * (c + 1)):
                        last = dve.bn_stats(stats2[:, i, :], y[:, T * b + i, :])
                    c_link(last)
                return step

            def c_ms(b, X):
                for i in range(T):
                    last = dve.bn_aggr(mv2[:, i, :], stats2[:, i, :])
                c_link(last)
                r = rms[:, bt[b]]
                c_link(dve.tensor_tensor(r, mv2[:, :, 0], mv2[:, :, 0], ALU.mult))
                dve.scalar_tensor_tensor(r, mv2[:, :, 1], EPS, r, ALU.add, ALU.add).then_inc(c_var, 1)

            def c_norm(c):
                def step(b, X):
                    dve.wait_ge(c_rms, b + 1)
                    for i in range(TC * c, TC * (c + 1)):
                        k = T * b + i
                        last = dve.tensor_scalar(h2[:, k, :], y[:, k, :], rms[:, k:k + 1], None, ALU.mult)
                    last.then_inc(c_h, 1)
                return step

            def c_lo_part(c):
                def step(b, X):
                    bs = slice(S * b + C2 * c, S * b + C2 * (c + 1))
                    dve.wait_ge(c_hi, 2 * b + c + 1)
                    dve.tensor_tensor(h2l[:, bs], h2t[:, bs], h2h[:, bs].bitcast(F),
                                      ALU.subtract).then_inc(c_lo, 1)
                return step

            def c_shift(b, X):
                dve.wait_ge(c_lg, b + 1)
                src = X[0][:, 0:T * E].rearrange("p (t e) -> p t e", t=T)
                c_link(dve.reduce_max(r8[:, 0, :], src, AX.X))
                dve.tensor_tensor(lg[:, :, :], src, r8[:, 0, :].unsqueeze(2).broadcast_to([P, T, E]),
                                  ALU.subtract).then_inc(c_sh, 1)

            f_of = ex[:, :, :].unsqueeze(2).broadcast_to([P, T, E, E])
            e_of = ex[:, :, :].unsqueeze(3).broadcast_to([P, T, E, E])

            def c_greater(b, X):
                dve.wait_ge(c_ex, b + 1)
                c_link(dve.tensor_tensor(cmp1[:, :, :, :], f_of, e_of, ALU.is_gt))

            def c_equal(b, X):
                c_link(dve.tensor_tensor(cmp2[:, :, :, :], f_of, e_of, ALU.is_equal))

            def c_before(b, X):
                c_link(dve.tensor_tensor(cmp2[:, :, :, :], cmp2[:, :, :, :],
                                         tri[:, :, :].unsqueeze(1).broadcast_to([P, T, E, E]), ALU.mult))

            def c_either(b, X):
                c_link(dve.tensor_tensor(cmp1[:, :, :, :], cmp1[:, :, :, :], cmp2[:, :, :, :], ALU.add))

            def c_rank(b, X):
                c_link(dve.reduce_sum(lg[:, :, :], cmp1[:, :, :, :], AX.X))

            def c_top2(b, X):
                c_link(dve.scalar_tensor_tensor(ex[:, :, :], lg[:, :, :], 1.5, ex[:, :, :], ALU.is_lt, ALU.mult))
                c_link(dve.reduce_sum(r8[:, 0, :], ex[:, :, :], AX.X))
                c_link(dve.reciprocal(r8[:, 1, :], r8[:, 0, :]))
                dve.tensor_tensor(gate_w[:, bt[b], :], ex[:, :, :],
                                  r8[:, 1, :].unsqueeze(2).broadcast_to([P, T, E]), ALU.mult).then_inc(c_w, 1)

            def c_gate_rows(c):
                def step(b, X):
                    dve.wait_ge(c_gt, 2 * b + c + 1)
                    dve.tensor_copy(gate_wt[b][:, C2 * c:C2 * (c + 1)], X[c][0:E, :]).then_inc(c_gc, 1)
                return step

            C_STEPS = [c_x2(0), c_x2(1), c_stats(0), c_stats(1), c_ms, c_norm(0), c_norm(1),
                       c_lo_part(0), c_lo_part(1), c_shift, c_greater, c_equal, c_before, c_either,
                       c_rank, c_top2, c_gate_rows(0), c_gate_rows(1)]

            def period(n, half, par, last=False, first=False):
                for item in ITEMS:
                    if item[0] == "e":
                        e = item[1]
                        if not isinstance(n, int) or issued(n + 1, e):
                            element(n + 1, half + par, 1 - par, e, idx(n + 1, e), bank_no(n + 1, e))
                    elif last and item[0] == "st" and item[2] == 1:
                        stage_c("dve", C_STEPS, 0, item[1])

            for e in range(NE):
                if issued(0, e):
                    element(0, 0, 0, e, idx(0, e), bank_no(0, e))
            period(0, 0, 0, first=True)
            with dve.Fori(0, 3) as it:
                period(1 + 2 * it, it, 1)
                period(2 + 2 * it, it + 1, 0)
            period(NG - 1, 3, 1, last=True)

            def sum_up(ch):
                xs = x[:, bass.ds(TC * ch, TC), :].rearrange("p t d -> p (t d)")
                ys = y[:, bass.ds(TC * ch, TC), :].rearrange("p t d -> p (t d)")
                dve.tensor_tensor(xs, xs, ys, ALU.add).then_inc(d_x, 1)
                dve.wait_ge(d_x, ch + 1)
                dve.wait_ge(d_tr, ch + 1)
                dve.tensor_tensor(xs, xs, obank[1][:, :], ALU.add).then_inc(d_acc, 1)

            def chunk(ch, first=False):
                for m in range(2 * E):
                    e = m // 2
                    dve.wait_ge(d_s, 2 * E * ch + m + 1)
                    if m % 2 == 0:
                        dve.wait_ge(ld_b[e % 4], 32 * ch + 16 * (e // 4 + 1))
                    dve.tensor_tensor(sw[m % 2][:, :], silu[m % 2][:, :], wbc[e % 4][:, :],
                                      ALU.mult).then_inc(d_sw, 1)
                    dve.wait_ge(d_u, 2 * E * ch + m + 1)
                    if not (first and m < 2):
                        dve.wait_ge(d_lo, 2 * E * ch + m - 1)
                    dve.wait_ge(d_sw, 2 * E * ch + m + 1)
                    dve.tensor_tensor(gg[m % 2][:, :], sw[m % 2][:, :], pair[m % 2][:, 0, :],
                                      ALU.mult).then_inc(d_g, 1)
                    if m == LAGD + 1 and not first:
                        sum_up(ch - 1)
                    if first and m == 1:
                        element(NG + 1, 4, 1, O1, idx(NG + 1, O1), bank_no(NG + 1, O1))
                    if isinstance(ch, int):
                        stage_c("dve", C_STEPS, 1, 2 * E * ch + m)

            chunk(0, first=True)
            chunk(1)
            with dve.Fori(2, B * NC_) as ch:
                chunk(ch)
            sum_up(B * NC_ - 1)

        @block.tensor
        def _(pe):
            pe.wait_ge(cst, 13)

            def transposes(b, n, banks):
                for c in range(NC_):
                    pe.wait_ge(a_h, 2 * n + c + 1)
                    for i in range(TC):
                        last = pe.transpose(banks[c][:, P * i:P * (i + 1)], h_a[b][:, TC * c + i, :],
                                            ident[:, :])
                    last.then_inc(a_tr, 1)

            for b in range(B):
                X = XA[b]
                for i in range(T):
                    if i % TC == 0:
                        pe.wait_ge(a_h, 2 * b + i // TC + 1)
                    last = pe.matmul(X[0][:, 0:HID], h_a[b][:, i, :], h_a[b][:, i, :],
                                     start=i == 0, stop=i == T - 1)
                last.then_inc(a_g, 1)
                transposes(b, b, X[1:3])
                if b == 0:
                    pe.wait_ge(ld_w, 16 * 6)
                pe.wait_ge(a_gs, b + 1)
                pe.matmul(X[3][:, 0:HID], qmat[:, :], g_sb[b][:, :], start=True,
                          stop=True).then_inc(a_m, 1)
                pe.wait_ge(a_ms, b + 1)
                for c in range(NC_):
                    pe.wait_ge(a_ht, 2 * b + c + 1)
                    for i in range(TC):
                        t = TC * c + i
                        last = pe.matmul(X[c][:, P * i:P * (i + 1)], ht_a[b][:, P * t:P * (t + 1)],
                                         m_sb[b][:, :], start=True, stop=True)
                    last.then_inc(a_att, 1)

            def project_k(b):
                X = XA[b]
                pe.wait_ge(a_ht, 2 * B + 2 * (b + 1))
                for bk, w0 in ((X[2], K0), (X[3], RK0)):
                    for c in range(NC_):
                        last = pe.matmul(bk[32 * c:32 * (c + 1), :], wqk_sb[:, w0:w0 + 32],
                                         ht_a[b][:, C2 * c:C2 * (c + 1)], start=True, stop=True)
                last.then_inc(a_qk[b], 1)

            def project_q(b, c):
                if c:
                    pe.wait_ge(a_mul, 3 * b + 1)
                for bk, w0 in ((XA[b][2 * c], QK0), (XA[b][2 * c + 1], RQ0)):
                    last = pe.matmul(bk, wqk_sb[:, w0:w0 + P], ht_a[b][:, C2 * c:C2 * (c + 1)],
                                     start=True, stop=True)
                last.then_inc(a_qk[b], 1)

            def project_v(b):
                pe.wait_ge(a_mul, 3 * b + 2)
                for i in range(T):
                    last = pe.matmul(XA[b][0][:, 32 * i:32 * (i + 1)], ht_a[b][:, P * i:P * (i + 1)],
                                     wqk_sb[:, V0:V0 + 32], start=True, stop=True)
                last.then_inc(a_v, 1)

            transposes(0, B, XA[0][2:4])
            project_k(0)
            project_q(0, 0)
            transposes(1, B + 1, XA[1][2:4])
            project_q(0, 1)
            project_v(0)
            project_k(1)
            project_q(1, 0)
            project_q(1, 1)
            project_v(1)

            pe.wait_ge(a_mul, 3)
            pe.wait_ge(a_vs, 1)

            def element(n, half, par, e, no, bk):
                kind, u = STREAM[e]
                bk = S_BANKS[bk]
                if isinstance(n, int) and n >= NG:
                    pe.wait_ge(s_free, no)
                elif not (isinstance(no, int) and no < NSB):
                    pe.wait_ge(s_free, no - NSB + 1)
                if kind == "s":
                    i, k0, nb, heads = u
                    w = nb * P
                    if UNIT_OF[e] == 0:
                        pe.wait_ge(ld_s[par], 16 * 8 * (half + 1))
                    diag = k0 + nb - 1 == i
                    nh = len(heads)
                    o = bk[:, 0:w * nh].rearrange("p (h k) -> p h k", h=nh)
                    last = pe.matmul(o, sq_stk[par][:, P * i:P * (i + 1)],
                                     sk_stk[par][:, heads[0]:heads[0] + nh, P * k0:P * k0 + w],
                                     start=True, stop=not diag)
                    if diag:
                        last = pe.matmul(o[:, :, w - P:w], ident_bf[:, :],
                                         mask_bf[:, :].unsqueeze(1).broadcast_to([P, nh, P]),
                                         start=False, stop=True)
                    last.then_inc(s_ready, 1)
                elif kind == "t":
                    g, c = (n, 0) if e == T0 else (n - 1, 1)
                    pe.wait_ge(m_neg, 2 * g + c + 1)
                    pe.transpose(bk[0:32, 0:P], neg[:, c, :, :, :].rearrange("p h s i -> p (h s i)"),
                                 ident[:, :]).then_inc(s_ready, 1)
                else:
                    g, c = (n - 1, 0) if e == O0 else (n - 2, 1)
                    pe.wait_ge(o_cp, 2 * g + c + 1)
                    for i in range(TC):
                        last = pe.transpose(bk[:, P * i:P * (i + 1)], o_sb[c][:, P * i:P * (i + 1)],
                                            ident[:, :])
                    last.then_inc(s_ready, 1)

            def times_v(n, par, s):
                c, j = SLOTS[s]
                q0, w = slot_cols(c, j)
                if DIAG[s]:
                    pe.wait_ge(k_done, NMASK * n + MASK_NO[s] + 2)
                pe.wait_ge(e_done, NU * n + 2 * s + 2)
                for r in range(REP):
                    last = pe.matmul(o_acc[32 * r:32 * (r + 1), q0:C2], v_stk[par][:, j, :],
                                     pt[:, (2 * s + r // 2) % NPB, r % 2, 0:w],
                                     start=j == 0, stop=j == TC * (c + 1) - 1)
                last.then_inc(pv_done, 1)

            def c_attn(b, X):
                pe.wait_ge(s_free, TAIL if b == 0 else len(_ORDER))
                if b == 1:
                    pe.wait_ge(e_done, NU * NG)
                for c in range(NC_):
                    for i in range(TC):
                        src = otok[:, TC * c + i, NKV * b:NKV * (b + 1), :].rearrange("p g d -> p (g d)")
                        last = pe.transpose(X[c][:, P * i:P * (i + 1)], src, ident[:, :])
                    last.then_inc(c_tr, 1)

            def c_wo_mm(b, X):
                for c in range(NC_):
                    pe.wait_ge(c_cp, 4 * b + c + 1)
                    for i in range(TC):
                        t = TC * c + i
                        last = pe.matmul(X[c][:, P * i:P * (i + 1)], ot[b][:, P * t:P * (t + 1)],
                                         wo_sb[:, :], start=True, stop=True)
                    last.then_inc(c_wo, 1)

            def c_h2_tr(b, X):
                for c in range(NC_):
                    pe.wait_ge(c_h, 2 * b + c + 1)
                    for i in range(TC):
                        last = pe.transpose(X[c][:, P * i:P * (i + 1)], h2[:, T * b + TC * c + i, :], ident[:, :])
                    last.then_inc(c_tr, 1)

            def c_logits(b, X):
                pe.wait_ge(c_cp, 4 * (b + 1))
                pe.wait_ge(c_hi, 2 * b + 1)
                for i in range(T):
                    last = pe.matmul(X[0][:, E * i:E * (i + 1)], h2t[:, S * b + P * i:S * b + P * (i + 1)],
                                     gate_sb[:, :], start=True, stop=True)
                last.then_inc(c_lg, 1)

            def c_gate_tr(b, X):
                pe.wait_ge(c_w, b + 1)
                pe.wait_ge(c_hi, 2 * (b + 1))
                for c in range(NC_):
                    for i in range(TC):
                        last = pe.transpose(X[c][0:E, P * i:P * (i + 1)], gate_w[:, T * b + TC * c + i, :],
                                            ident[:, :])
                    last.then_inc(c_gt, 1)

            C_STEPS = [c_attn, c_wo_mm, c_h2_tr, c_logits, c_gate_tr]

            def period(n, half, par, first=False, last=False):
                for item in ITEMS:
                    kind, s = item[0], item[1]
                    if kind == "e":
                        if not isinstance(n, int) or issued(n + 1, s):
                            element(n + 1, half + par, 1 - par, s, idx(n + 1, s), bank_no(n + 1, s))
                    elif kind == "st":
                        t = item[2]
                        c, j = SLOTS[s]
                        q0, w = slot_cols(c, j)
                        if s == 0 and t == 0:
                            pe.wait_ge(ld_t[par], 16 * 7 * (half + 1))
                        if j == 0 and t == 0:
                            pe.wait_ge(ld_m[c][par], 64 * (half + 1))
                        v = 2 * s + t
                        if not (first and v < 2):
                            pe.wait_ge(e_done, NU * n + v - 1)
                        for jj in range(2):
                            ins = pe.matmul(pair[v % 2][:, jj, 0:w], tk_stk[par][64 * jj:64 * jj + 34, P * j:P * (j + 1)],
                                            tq_stk[par][t][64 * jj:64 * jj + 34, C2 * c + q0:C2 * (c + 1)],
                                            start=True, stop=True)
                        ins.then_inc(t_done, 1)
                        if last and t == 1:
                            stage_c("pe", C_STEPS, 0, s)
                    elif kind == "pv":
                        if s >= LAG:
                            if s - LAG == 0 and not first:
                                pe.wait_ge(o_cp, 2 * n)
                            if s - LAG == TC:
                                pe.wait_ge(o_cp, 2 * n + 1)
                            times_v(n, par, s - LAG)
                        elif not first:
                            times_v(n - 1, 1 - par, NS - LAG + s)

            for e in range(NE):
                if issued(0, e):
                    element(0, 0, 0, e, idx(0, e), bank_no(0, e))
            pe.wait_ge(cst, 17)
            pe.wait_ge(a_mul, 3 * B)
            pe.wait_ge(a_vs, B)
            period(0, 0, 0, first=True)
            with pe.Fori(0, 3) as it:
                period(1 + 2 * it, it, 1)
                period(2 + 2 * it, it + 1, 0)
            period(NG - 1, 3, 1, last=True)
            for s in range(NS - LAG, NS):
                times_v(NG - 1, 1, s)

            pe.wait_ge(w_lo, 3)
            pe.wait_ge(c_lo, 2)
            pe.wait_ge(c_gc, 2)

            def down(ch, m):
                e, f = m // 2, m % 2
                pe.wait_ge(d_hi, 2 * E * ch + m + 1)
                for w in (w2h, w2l):
                    pe.matmul(obank[0][:, :], w[:, e, f, :], gh[m % 4][:, :], start=m == 0 and w is w2h,
                              stop=False)
                pe.wait_ge(d_lo, 2 * E * ch + m + 1)
                pe.matmul(obank[0][:, :], w2h[:, e, f, :], gl[m % 4][:, :], start=False,
                          stop=m == 2 * E - 1).then_inc(d_dn, 1)

            def sum_transposes(ch):
                pe.wait_ge(d_o, ch + 1)
                for i in range(TC):
                    last = pe.transpose(obank[1][:, P * i:P * (i + 1)], out_t[:, P * i:P * (i + 1)], ident[:, :])
                last.then_inc(d_tr, 1)

            def chunk(ch, first=False):
                for m in range(2 * E):
                    for which, bk, free, ready in ((0, bank[m % 2][:, :], d_s, d_a),
                                                   (1, pair[m % 2][:, 0, :], d_g, d_u)):
                        if not (first and m < 2):
                            pe.wait_ge(free, 2 * E * ch + m - 1)
                        col = which * FFN + m % 2 * P
                        for k, (w, h) in enumerate(((w13h, h2h), (w13h, h2l), (w13l, h2h))):
                            last = pe.matmul(bk, w[:, m // 2, col:col + P], h[:, bass.ds(C2 * ch, C2)],
                                             start=k == 0, stop=k == 2)
                        last.then_inc(ready, 1)
                    if m >= LAGD:
                        if m == LAGD:
                            if first:
                                pe.wait_ge(o_cp, 2 * NG)
                            else:
                                pe.wait_ge(d_o, ch)
                        down(ch, m - LAGD)
                    elif not first:
                        down(ch - 1, 2 * E - LAGD + m)
                    if m == LAGD and not first:
                        sum_transposes(ch - 1)
                    if first and m == 0:
                        element(NG + 1, 4, 1, O1, idx(NG + 1, O1), bank_no(NG + 1, O1))
                    if isinstance(ch, int):
                        stage_c("pe", C_STEPS, 1, 2 * E * ch + m)

            chunk(0, first=True)
            chunk(1)
            pe.wait_ge(c_lo, 2 * B)
            with pe.Fori(2, B * NC_) as ch:
                chunk(ch)
            for m in range(2 * E - LAGD, 2 * E):
                down(B * NC_ - 1, m)
            sum_transposes(B * NC_ - 1)

    return nc


_INS = ["L0_attn_hidden_states", "L0_attn_queries", "L0_ffn_ln1_w", "L0_ffn_ln2_w", "L0_ffn_wqkv",
        "L0_ffn_wo", "L0_ffn_gate_w", "L0_ffn_w13", "L0_ffn_w2"]


def _rope_tables():
    import numpy as np
    inv = (np.float32(1.0) / np.float32(10000.0) ** (np.arange(0, HD, 2, dtype=np.float32) / np.float32(HD)))
    ang = np.arange(S, dtype=np.float32)[:, None] * inv.astype(np.float32)[None, :]
    ang = np.concatenate([ang, ang], axis=1).T
    cos, sin = np.cos(ang).astype(np.float32), np.sin(ang).astype(np.float32)
    sin = sin * np.where(np.arange(HD) < HD // 2, -1.0, 1.0).astype(np.float32)[:, None]
    scale = np.float32(HD ** -0.5)
    cq, sq = np.tile(cos * scale, (NH, 1)), np.tile(sin * scale, (NH, 1))

    def halves(a):
        a = np.tile(a, (NKV, 1))
        return np.concatenate([a[:, C2 * c:C2 * (c + 1)] for c in range(NC_)], axis=0)
    return [np.ascontiguousarray(a, dtype=np.float32) for a in (cq, sq, halves(cos), halves(sin))]


def kernel(**inputs):
    import numpy as np
    import concourse.bacc as bacc
    from concourse.bass_utils import run_bass_kernel_spmd

    a = {k: np.asarray(inputs[k]) for k in _INS}
    turned = (np.arange(HD) + HD // 2) % HD
    w = a["L0_ffn_wqkv"].T
    nq, nk = NH * HD, NKV * HD
    wq, wk, wv = w[:, :nq], w[:, nq:nq + nk], w[:, nq + nk:]
    wrq = wq.reshape(HID, NH, HD)[:, :, turned].reshape(HID, nq)
    wrk = wk.reshape(HID, NKV, HD)[:, :, turned].reshape(HID, nk)
    arrays = {
        "x_in": a["L0_attn_hidden_states"],
        "queries": a["L0_attn_queries"],
        "ln1": a["L0_ffn_ln1_w"].reshape(HID, 1),
        "ln2": a["L0_ffn_ln2_w"].reshape(HID, 1),
        "wqk": np.concatenate([wq, wrq, wk, wrk, wv], axis=1),
        "wo_t": a["L0_ffn_wo"].T,
        "gate_t": a["L0_ffn_gate_w"].T,
        "w13_t": a["L0_ffn_w13"].transpose(0, 2, 1),
        "w2_t": a["L0_ffn_w2"].transpose(0, 2, 1),
    }
    for name, table in zip(("cos_q", "sin_q", "cos_k", "sin_k"), _rope_tables()):
        arrays[name] = table
    arrays = {k: np.ascontiguousarray(v) for k, v in arrays.items()}
    nc = bacc.Bacc("TRN2", target_bir_lowering=False, num_devices=1)
    args = [nc.dram_tensor(k, v.shape, mybir.dt.from_np(v.dtype), kind="ExternalInput").ap()
            for k, v in arrays.items()]
    args.append(nc.dram_tensor("result", (B, S, HID), mybir.dt.float32, kind="ExternalOutput").ap())
    build_program(nc, *args)
    r = run_bass_kernel_spmd(nc, [arrays], core_ids=[0])
    return r.results[0]["result"]
```
